# Optimizing a Trainium2 kernel written in Bass

```python
import numpy as np
import jax
import jax.numpy as jnp

def _softmax(x, axis=-1):
    return jax.nn.softmax(x, axis=axis)
def _gelu(x):
    return jax.nn.gelu(x, approximate=True)
def _silu(x):
    return jax.nn.silu(x)
def _sigmoid(x):
    return jax.nn.sigmoid(x)
def _layernorm(x, axis=-1, eps=1e-5):
    m = jnp.mean(x, axis=axis, keepdims=True)
    v = jnp.var(x, axis=axis, keepdims=True)
    return (x - m) / jnp.sqrt(v + eps)
def _scatter_add(tgt, idx, src, axis=0):
    return tgt.at[idx].add(src)
def _segment_sum(src, seg, n):
    return jax.ops.segment_sum(src, seg, n)

kernel_name = 'mk_conv_preact_d2_conv_nhwc96_e7bc7b'

def setup_inputs(seed: int = 0):
    np.random.seed(seed)
    _w = jnp.asarray
    def _rec_inputs():
        import jax
        import jax.numpy as jnp
        _gk = jax.random.key(seed)
        x = -0.0001538 + 1 * jax.random.normal(jax.random.fold_in(_gk, 1), (16, 64, 64, 96), jnp.float32)
        return x
    x = _rec_inputs()
    def _L0_conv_setup():
        import jax, jax.numpy as jnp
        import numpy as np
        UP = 2

        def _rect_1d(N, cutoff, edge_val):
            lo = int(N * cutoff // 2)
            hi = int(N - lo)
            r = np.ones(N, dtype=np.float32)
            r[lo + 1:hi] = 0.0
            if cutoff * N % 2 == 0:
                r[lo] = edge_val
                r[hi] = edge_val
            return r

        def _rect_mask_rfft(N, cutoff, edge_val):
            r = _rect_1d(N, cutoff, edge_val)
            m = r[:, None] * r[None, :]
            return jnp.asarray(m[:, :N // 2 + 1])

        def _upsample_rfft(x):
            B, C, H, W = x.shape
            z = jnp.zeros((B, C, H, UP, W, UP), x.dtype)
            z = z.at[:, :, :, 0, :, 0].set(x)
            xu = z.reshape(B, C, H * UP, W * UP)
            mask = _rect_mask_rfft(W * UP, 1.0 / UP, 1.0)
            xf = jnp.fft.rfft2(xu) * (UP * UP) * mask
            return jnp.fft.irfft2(xf, s=(H * UP, W * UP)).astype(x.dtype)

        def _lpf_rfft(x, cutoff=0.5):
            H, W = (x.shape[-2], x.shape[-1])
            mask = _rect_mask_rfft(W, cutoff, 0.5)
            xf = jnp.fft.rfft2(x) * mask
            return jnp.fft.irfft2(xf, s=(H, W)).astype(x.dtype)
        key = jax.random.key(seed)
        ks = jax.random.split(key, 6)
        B, H, W, dim = (16, 64, 64, 96)
        hidden = 4 * dim
        x = jax.random.normal(ks[0], (B, H, W, dim), jnp.float32)
        W1 = jax.random.normal(ks[1], (hidden, dim), jnp.float32) * 0.02
        b1 = jnp.zeros((hidden,), jnp.float32)
        W2 = jax.random.normal(ks[2], (dim, hidden), jnp.float32) * 0.02
        b2 = jnp.zeros((dim,), jnp.float32)
        init_coef = jnp.asarray([0.0169394634313126, 0.5, 0.3078363963999393], jnp.float32)
        coef = jnp.tile(init_coef[None, :], (hidden, 1))
        return {'x': x, 'W1': W1, 'b1': b1, 'W2': W2, 'b2': b2, 'coef': coef}
    _L0_conv_all = _L0_conv_setup()
    _L0_conv_in = {k: v for k, v in _L0_conv_all.items() if k in ('W1', 'b1', 'W2', 'b2', 'coef', )}
    del _L0_conv_all

    def _L1_conv_setup():
        import jax, jax.numpy as jnp
        import numpy as np
        D_MODEL = 96
        D_INNER = 192
        R = 6
        DH = 32
        K = 4
        N = 16
        EPS = 1e-05

        def _cross_scan(x):
            B, H, W, C = x.shape
            x0 = x.reshape(B, H * W, C)
            x1 = jnp.transpose(x, (0, 2, 1, 3)).reshape(B, H * W, C)
            return jnp.stack([x0, x1, x0[:, ::-1], x1[:, ::-1]], axis=2)

        def _cross_merge(ys, H, W):
            B, L, _, C = ys.shape
            y_row = ys[:, :, 0] + ys[:, :, 2][:, ::-1]
            y_col = ys[:, :, 1] + ys[:, :, 3][:, ::-1]
            y_col = jnp.transpose(y_col.reshape(B, W, H, C), (0, 2, 1, 3)).reshape(B, L, C)
            return y_row + y_col

        def _selective_scan(us, dts, As, Bs, Cs, Dsr, dtb):
            dt = jax.nn.softplus(dts + dtb)
            decay = jnp.exp(dt * As)
            xu = dt[..., None] * us
            Bh = jnp.repeat(Bs, R, axis=2)
            Ch = jnp.repeat(Cs, R, axis=2)
            B_, L, KR, _ = us.shape
            tfirst = lambda a: jnp.moveaxis(a, 1, 0)

            def step(h, inp):
                dec, xu_t, b_t, c_t = inp
                h = dec[:, :, None, None] * h + xu_t[..., None] * b_t[:, :, None, :]
                y = jnp.einsum('bkdn,bkn->bkd', h, c_t)
                return (h, y)
            h0 = jnp.zeros((B_, KR, DH, N), us.dtype)
            _, ys = jax.lax.scan(step, h0, (tfirst(decay), tfirst(xu), tfirst(Bh), tfirst(Ch)))
            ys = jnp.moveaxis(ys, 0, 1)
            return ys + us * Dsr
        key = jax.random.key(seed)
        ks = jax.random.split(key, 10)
        B, H, W = (8, 64, 64)
        f = lambda k, s, sc: jax.random.normal(k, s, jnp.float32) * sc
        return dict(x=jax.random.normal(ks[0], (B, H, W, D_MODEL), jnp.float32), w_in=f(ks[1], (D_MODEL, D_INNER), 0.02), w_conv=f(ks[2], (3, 3, 1, D_INNER), 0.1), b_conv=f(ks[3], (D_INNER,), 0.1), x_proj_weight=f(ks[4], (K, R + 2 * N, D_INNER), 0.02), A_logs=f(ks[5], (K, R), 0.5), Ds=jnp.ones((K, R, DH), jnp.float32), dt_bias=0.1 * jax.random.uniform(ks[6], (K, R), jnp.float32), ln_g=jnp.ones((D_INNER,), jnp.float32), ln_b=jnp.zeros((D_INNER,), jnp.float32), w_out=f(ks[7], (D_INNER, D_MODEL), 0.02))
    _L1_conv_all = _L1_conv_setup()
    _L1_conv_in = {k: v for k, v in _L1_conv_all.items() if k in ('w_in', 'w_conv', 'b_conv', 'x_proj_weight', 'A_logs', 'Ds', 'dt_bias', 'ln_g', 'ln_b', 'w_out', )}
    del _L1_conv_all

    return {
        "x": x,
        "L0_conv_W1": _L0_conv_in["W1"],
        "L0_conv_b1": _L0_conv_in["b1"],
        "L0_conv_W2": _L0_conv_in["W2"],
        "L0_conv_b2": _L0_conv_in["b2"],
        "L0_conv_coef": _L0_conv_in["coef"],
        "L1_conv_w_in": _L1_conv_in["w_in"],
        "L1_conv_w_conv": _L1_conv_in["w_conv"],
        "L1_conv_b_conv": _L1_conv_in["b_conv"],
        "L1_conv_x_proj_weight": _L1_conv_in["x_proj_weight"],
        "L1_conv_A_logs": _L1_conv_in["A_logs"],
        "L1_conv_Ds": _L1_conv_in["Ds"],
        "L1_conv_dt_bias": _L1_conv_in["dt_bias"],
        "L1_conv_ln_g": _L1_conv_in["ln_g"],
        "L1_conv_ln_b": _L1_conv_in["ln_b"],
        "L1_conv_w_out": _L1_conv_in["w_out"],
    }

def reference(x, L0_conv_W1, L0_conv_b1, L0_conv_W2, L0_conv_b2, L0_conv_coef, L1_conv_w_in, L1_conv_w_conv, L1_conv_b_conv, L1_conv_x_proj_weight, L1_conv_A_logs, L1_conv_Ds, L1_conv_dt_bias, L1_conv_ln_g, L1_conv_ln_b, L1_conv_w_out):
    import jax
    import jax.numpy as jnp
    def _L0_conv_ref(x, W1, b1, W2, b2, coef):
        import jax, jax.numpy as jnp
        import numpy as np
        UP = 2

        def _rect_1d(N, cutoff, edge_val):
            lo = int(N * cutoff // 2)
            hi = int(N - lo)
            r = np.ones(N, dtype=np.float32)
            r[lo + 1:hi] = 0.0
            if cutoff * N % 2 == 0:
                r[lo] = edge_val
                r[hi] = edge_val
            return r

        def _rect_mask_rfft(N, cutoff, edge_val):
            r = _rect_1d(N, cutoff, edge_val)
            m = r[:, None] * r[None, :]
            return jnp.asarray(m[:, :N // 2 + 1])

        def _upsample_rfft(x):
            B, C, H, W = x.shape
            z = jnp.zeros((B, C, H, UP, W, UP), x.dtype)
            z = z.at[:, :, :, 0, :, 0].set(x)
            xu = z.reshape(B, C, H * UP, W * UP)
            mask = _rect_mask_rfft(W * UP, 1.0 / UP, 1.0)
            xf = jnp.fft.rfft2(xu) * (UP * UP) * mask
            return jnp.fft.irfft2(xf, s=(H * UP, W * UP)).astype(x.dtype)

        def _lpf_rfft(x, cutoff=0.5):
            H, W = (x.shape[-2], x.shape[-1])
            mask = _rect_mask_rfft(W, cutoff, 0.5)
            xf = jnp.fft.rfft2(x) * mask
            return jnp.fft.irfft2(xf, s=(H, W)).astype(x.dtype)
        xc = jnp.transpose(x, (0, 3, 1, 2))
        xu = _upsample_rfft(xc)
        h = jnp.transpose(xu, (0, 2, 3, 1))
        h = h @ W1.T + b1
        h = coef[:, 0] + coef[:, 1] * h + coef[:, 2] * (h * h)
        h = h @ W2.T + b2
        hc = jnp.transpose(h, (0, 3, 1, 2))
        hl = _lpf_rfft(hc, cutoff=0.5)
        out = hl[:, :, ::2, ::2]
        return jnp.transpose(out, (0, 2, 3, 1))

    def _L1_conv_ref(x, w_in, w_conv, b_conv, x_proj_weight, A_logs, Ds, dt_bias, ln_g, ln_b, w_out):
        import jax, jax.numpy as jnp
        import numpy as np
        D_MODEL = 96
        D_INNER = 192
        R = 6
        DH = 32
        K = 4
        N = 16
        EPS = 1e-05

        def _cross_scan(x):
            B, H, W, C = x.shape
            x0 = x.reshape(B, H * W, C)
            x1 = jnp.transpose(x, (0, 2, 1, 3)).reshape(B, H * W, C)
            return jnp.stack([x0, x1, x0[:, ::-1], x1[:, ::-1]], axis=2)

        def _cross_merge(ys, H, W):
            B, L, _, C = ys.shape
            y_row = ys[:, :, 0] + ys[:, :, 2][:, ::-1]
            y_col = ys[:, :, 1] + ys[:, :, 3][:, ::-1]
            y_col = jnp.transpose(y_col.reshape(B, W, H, C), (0, 2, 1, 3)).reshape(B, L, C)
            return y_row + y_col

        def _selective_scan(us, dts, As, Bs, Cs, Dsr, dtb):
            dt = jax.nn.softplus(dts + dtb)
            decay = jnp.exp(dt * As)
            xu = dt[..., None] * us
            Bh = jnp.repeat(Bs, R, axis=2)
            Ch = jnp.repeat(Cs, R, axis=2)
            B_, L, KR, _ = us.shape
            tfirst = lambda a: jnp.moveaxis(a, 1, 0)

            def step(h, inp):
                dec, xu_t, b_t, c_t = inp
                h = dec[:, :, None, None] * h + xu_t[..., None] * b_t[:, :, None, :]
                y = jnp.einsum('bkdn,bkn->bkd', h, c_t)
                return (h, y)
            h0 = jnp.zeros((B_, KR, DH, N), us.dtype)
            _, ys = jax.lax.scan(step, h0, (tfirst(decay), tfirst(xu), tfirst(Bh), tfirst(Ch)))
            ys = jnp.moveaxis(ys, 0, 1)
            return ys + us * Dsr
        B, H, W, _ = x.shape
        L = H * W
        xi = x @ w_in
        xi = jax.lax.conv_general_dilated(xi, w_conv, (1, 1), 'SAME', feature_group_count=D_INNER, dimension_numbers=('NHWC', 'HWIO', 'NHWC')) + b_conv
        xi = jax.nn.silu(xi)
        xs = _cross_scan(xi)
        x_dbl = jnp.einsum('blkd,kcd->blkc', xs, x_proj_weight)
        dts = x_dbl[..., :R].reshape(B, L, K * R)
        Bs = x_dbl[..., R:R + N]
        Cs = x_dbl[..., R + N:]
        us = xs.reshape(B, L, K * R, DH)
        As = -jnp.exp(A_logs.astype(jnp.float32)).reshape(K * R)
        Dsr = Ds.reshape(K * R, DH)
        dtb = dt_bias.reshape(K * R)
        ys = _selective_scan(us, dts, As, Bs, Cs, Dsr, dtb)
        y = _cross_merge(ys.reshape(B, L, K, R * DH), H, W)
        mu = y.mean(-1, keepdims=True)
        var = ((y - mu) ** 2).mean(-1, keepdims=True)
        y = (y - mu) / jnp.sqrt(var + EPS) * ln_g + ln_b
        y = y.reshape(B, H, W, D_INNER)
        return y @ w_out

    def _gn(v, G=32, eps=1e-5):
        B_, H_, W_, C_ = v.shape
        g = v.reshape(B_, H_, W_, G, C_ // G)
        m = jnp.mean(g, axis=(1, 2, 4), keepdims=True)
        s = jnp.var(g, axis=(1, 2, 4), keepdims=True)
        return ((g - m) / jnp.sqrt(s + eps)).reshape(v.shape)

    def _ln_c(v, eps=1e-6):
        m = jnp.mean(v, axis=-1, keepdims=True)
        s = jnp.var(v, axis=-1, keepdims=True)
        return (v - m) / jnp.sqrt(s + eps)

    def _ln_t(v, eps=1e-5):
        m = jnp.mean(v, axis=-1, keepdims=True)
        s = jnp.var(v, axis=-1, keepdims=True)
        return (v - m) / jnp.sqrt(s + eps)

    def _to_tokens(v):
        B_, H_, W_, C_ = v.shape
        return v.reshape(B_, H_ * W_, C_)
    def _from_tokens(t, like):
        return t.reshape(like.shape)

    x = x + _L0_conv_ref(_gn(x), L0_conv_W1, L0_conv_b1, L0_conv_W2, L0_conv_b2, L0_conv_coef)
    x = x + _L1_conv_ref(_gn(x), L1_conv_w_in, L1_conv_w_conv, L1_conv_b_conv, L1_conv_x_proj_weight, L1_conv_A_logs, L1_conv_Ds, L1_conv_dt_bias, L1_conv_ln_g, L1_conv_ln_b, L1_conv_w_out)
    return x


_drawn_inputs = setup_inputs


def setup_inputs(seed=0):
    import zlib

    import numpy as np

    out = dict(_drawn_inputs(seed))
    spreads = {'L0_conv_b1': (0.0, 0.37),
     'L0_conv_b2': (0.0, 0.1),
     'L1_conv_Ds': (1.0, 0.564),
     'L1_conv_ln_g': (1.0, 0.2),
     'L1_conv_ln_b': (0.0, 0.296)}
    factors = {'L1_conv_x_proj_weight': 8.0, 'L1_conv_A_logs': 8.0, 'L1_conv_dt_bias': 8.0}
    for name, (base, spread) in spreads.items():
        noise = np.random.default_rng([zlib.crc32(name.encode()), seed]).standard_normal(out[name].shape)
        drawn = base * np.exp(spread * noise) if base else spread * noise
        out[name] = jnp.asarray(drawn.astype(out[name].dtype))
    for name, factor in factors.items():
        out[name] = (out[name] * factor).astype(out[name].dtype)
    return out
```

```python
from contextlib import ExitStack

import concourse.bass as bass
from concourse import mybir

F32 = mybir.dt.float32
ALU = mybir.AluOpType
ACT = mybir.ActivationFunctionType

B, H, W, C = 16, 64, 64, 96
L = H * W
GROUP = 3
HID = 4 * C
KH = HID // 128
GRID = 96
DI = 192
HALF = 2
R, DH, N = 6, 32, 16
RH = R // HALF
Q = 64
NC = L // Q
NT = R + 4 * N
SLOT = NC + 1
NST = HALF * DH * SLOT + 1
NROW = 4
NTILE = GRID // NROW
PERBANK = 5
NJOB = -(-C // PERBANK)
NBLK = L // 128
GBLK = 4
NG = NBLK // GBLK

CONST_PARTS = [("up", GRID), ("down", W), ("ident", 128), ("fold", Q), ("after", 128), ("upto", 128),
               ("dirsum", C), ("tri", Q), ("group", C), ("headsel", RH), ("fwd", 1), ("bwd", 1),
               ("mean192", C), ("ones", 128), ("col192", 1)]
CONST_AT, CONST_N = {}, 0
for _name, _n in CONST_PARTS:
    CONST_AT[_name] = (CONST_N, CONST_N + _n)
    CONST_N += _n


def build(nc, a, out, images=B, dump=None):
    ctx = ExitStack()
    with ctx:
        def sb(name, n, dt=F32):
            return ctx.enter_context(nc.sbuf_tensor(name, [128, n], dt))

        def sem(name):
            return ctx.enter_context(nc.semaphore(name))

        bank = [ctx.enter_context(nc.psum_tensor(f"bank{i}", [128, 512], F32)) for i in range(8)]

        cst = sb("cst", CONST_N)
        K = {k: cst[:, s:e] for k, (s, e) in CONST_AT.items()}
        w1n = sb("w1n", KH * C)[:, :].rearrange("p (k c) -> p k c", k=KH)
        w1t = sb("w1t", HID)
        w1s = sb("w1s", HID)
        w2t = sb("w2t", KH * C)[:, :].rearrange("p (k c) -> p k c", k=KH)
        w2s = sb("w2s", KH * C)[:, :].rearrange("p (k c) -> p k c", k=KH)
        w2l = sb("w2l", KH * C)[:, :].rearrange("p (k c) -> p k c", k=KH)
        lin = sb("lin", C)
        lins = sb("lins", C)
        coef = sb("coef", KH * 3)[:, :].rearrange("p (k c) -> p k c", k=KH)
        b1 = sb("b1", KH)
        vconst = sb("vconst", KH)
        b2 = sb("b2", 1)
        out0 = sb("out0", 1)
        win = sb("win", DI)
        wins = sb("wins", DI)
        wconv = sb("wconv", HALF * 9)[:, :].rearrange("p (g t) -> p g t", g=HALF)
        bconv = sb("bconv", HALF)
        nbconv = sb("nbconv", HALF)
        wtok = sb("wtok", 2 * 2 * HALF * NT)[:, :].rearrange("p (o d g n) -> p o d g n", o=2, d=2, g=HALF)
        dtb = sb("dtb", 2 * R)[:, :].rearrange("p (o r) -> p o r", o=2)
        aneg = sb("aneg", 2 * R)[:, :].rearrange("p (o r) -> p o r", o=2)
        dsk = sb("dsk", HALF * 4)[:, :].rearrange("p (g k) -> p g k", g=HALF)
        dsum = sb("dsum", HALF)
        lng = sb("lng", HALF)
        lnb = sb("lnb", HALF)
        wout = sb("wout", HALF * C)[:, :].rearrange("p (g c) -> p g c", g=HALF)
        woutc = sb("woutc", HALF * (C + 1))[:, :].rearrange("p (g c) -> p g c", g=HALF)
        brow = sb("brow", C)
        bn = sb("bn", 8 * 6)[:, :].rearrange("p (k s) -> p k s", s=6)
        mv = sb("mv", 2)
        mom = sb("mom", 2)
        gst = sb("gst", 2)
        gsq = sb("gsq", 1)
        gvar = sb("gvar", 1)
        rstd = sb("rstd", 1)
        nmr = sb("nmr", 1)
        bias1 = sb("bias1", KH)
        out0i = sb("out0i", 1)
        biasin = sb("biasin", HALF)
        dtraw, expn, onep, den, tiny = (sb(n, NC * R) for n in ("dtraw", "expn", "onep", "den", "tiny"))
        dt = sb("dt", NC * R)
        aa = sb("aa", NC * R)
        wsuf = sb("wsuf", NC * R)
        ecum = sb("ecum", NC * R)
        tot = sb("tot", NC * R)
        dec = sb("dec", HALF * NC)
        xT = sb("xT", L)
        ARENA = 39700
        arena = sb("arena", ARENA)
        at = [0]

        def take(n, start=None):
            if start is not None:
                at[0] = start
            v = arena[:, at[0]:at[0] + n]
            at[0] += n
            assert at[0] <= ARENA, at
            return v

        xs = take(W * C, 0)
        y1 = xs
        st_a = take(GRID * C)
        z = st_a
        xu = take(GRID * GRID)
        sq = take(2 * KH * NROW * GRID).rearrange("p (s k n) -> p s k n", s=2, k=KH)
        PW = W + 2
        u = take(HALF * L, 0)
        y = take(HALF * L)
        etmp = y
        state_at = at[0]
        hf = take(NST)
        hb = take(NST)
        tokp = take(NC * NT)
        gm_at = at[0]
        xpad = take(HALF * PW * PW, state_at)
        ysq = take(HALF * L, state_at)
        gm = take(NC * Q, gm_at)
        uc = take(2 * HALF * Q).rearrange("p (s g t) -> p s g t", s=2, g=HALF)
        tk = take(2 * NT).rearrange("p (s n) -> p s n", s=2)
        bct = take(2 * 3 * Q).rearrange("p (s n) -> p s n", s=2)
        bh = take(2 * R * 2 * N).rearrange("p (s r n) -> p s r n", s=2, r=R)
        up = take(4 * R * DH).rearrange("p (s n) -> p s n", s=4)
        ring_at = at[0]
        rr = take(2 * R * Q).rearrange("p (s n) -> p s n", s=2)
        ee = take(2 * R * Q).rearrange("p (s n) -> p s n", s=2)
        mk = take(2 * R * Q).rearrange("p (s n) -> p s n", s=2)
        ct = take(2 * R * 2 * N).rearrange("p (s r n) -> p s r n", s=2, r=R)
        ch = take(4 * HALF * Q).rearrange("p (s g t) -> p s g t", s=4, g=HALF)
        hbd = take(4 * HALF * C).rearrange("p (s g n) -> p s g n", s=4, g=HALF)
        decx = take(NST, ring_at)
        xsb = take(2 * GBLK * C, ring_at).rearrange("p (s n) -> p s n", s=2)
        lns = take(2 * 4 * GBLK).rearrange("p (s i n) -> p s i n", s=2, i=4)
        ot = take(NBLK * C, gm_at)

        xs3 = xs[0:H, :].rearrange("p (w c) -> p w c", w=W)
        sta3 = st_a[0:W, :].rearrange("p (c h) -> p c h", c=C)
        xu3 = xu[0:C, :].rearrange("p (h w) -> p h w", h=GRID)
        z3 = z[0:GRID, :].rearrange("p (h c) -> p h c", h=GRID)
        y13 = y1[0:GRID, :].rearrange("p (c w) -> p c w", c=C)
        xT3 = xT[0:C, :].rearrange("p (h w) -> p h w", h=H)
        u4 = u[0:C, :].rearrange("p (g h w) -> p g h w", g=HALF, h=H)
        y4 = y[0:C, :].rearrange("p (g h w) -> p g h w", g=HALF, h=H)
        xp4 = xpad[0:C, :].rearrange("p (g h w) -> p g h w", g=HALF, h=PW)
        tok3 = tokp.rearrange("p (c n) -> p c n", c=NC)
        gm3 = gm.rearrange("p (c t) -> p c t", c=NC)

        def rc(t):
            return t[:, :].rearrange("p (c r) -> p c r", c=NC)

        def states(t, shift=0):
            return t[0:C, shift:shift + HALF * DH * SLOT].rearrange("p (n c) -> p n c", c=SLOT)

        def one(c):
            return slice(c, c + 1) if isinstance(c, int) else bass.ds(c, 1)

        def chunk(t4, o, c):
            v = t4[:, :, one(c), :] if o == 0 else t4[:, :, :, one(c)]
            return v.rearrange("p g a b -> p g (a b)")

        loads, x_in, u_free, stored = sem("loads"), sem("x_in"), sem("u_free"), sem("stored")
        waited = sem("waited")
        phase_done = sem("phase_done")
        dve_own, act_own = sem("dve_own"), sem("act_own")
        w2_scaled, folded, anegexp = sem("w2_scaled"), sem("folded"), sem("anegexp")
        mom_ready, grp_ready, var_ready = sem("mom_ready"), sem("grp_ready"), sem("var_ready")
        rstd_ready, nmr_ready, shift_ready = sem("rstd_ready"), sem("nmr_ready"), sem("shift_ready")
        tr_ready, tr_read = sem("tr_ready"), sem("tr_read")
        job_ready, job_act, job_dve, job_add = sem("job_ready"), sem("job_act"), sem("job_dve"), sem("job_add")
        hid_ready, hid_sq, proj_ready, proj_read = sem("hid_ready"), sem("hid_sq"), sem("proj_ready"), sem("proj_read")
        in_ready, in_read, conv_done, exp_done = sem("in_ready"), sem("in_read"), sem("conv_done"), sem("exp_done")
        abs_ready, spe_ready, onep_ready, ln_ready = sem("abs_ready"), sem("spe_ready"), sem("onep_ready"), sem("ln_ready")
        aa_ready, cum_ready, cum_exp = sem("aa_ready"), sem("cum_ready"), sem("cum_exp")
        uc_ready = sem("uc_ready")
        tok_ready, tok_out, tok_kept = sem("tok_ready"), sem("tok_out"), sem("tok_kept")
        bct_ready, bct_in, g_ready, g_read = sem("bct_ready"), sem("bct_in"), sem("g_ready"), sem("g_read")
        ut_ready, up_ready = sem("ut_ready"), sem("up_ready")
        bh_ready, dh_ready, dh_read = sem("bh_ready"), sem("dh_ready"), sem("dh_read")
        r_ready, d_ready, e_ready, m_ready = sem("r_ready"), sem("d_ready"), sem("e_ready"), sem("m_ready")
        ct_ready, c_ready, ch_ready = sem("ct_ready"), sem("c_ready"), sem("ch_ready")
        hbd_ready, yc_ready, y_added = sem("hbd_ready"), sem("yc_ready"), sem("y_added")
        fin_ready, fin_x, fin_var, fin_ln, fin_rstd = (sem(n) for n in ("fin_ready", "fin_x", "fin_var", "fin_ln", "fin_rstd"))
        fin_done, sq_ready = sem("fin_done"), sem("sq_ready")

        ENGINES = 4
        PHASES = 16
        JOBS = 2 * NJOB + 12 + 8
        NLOAD = 26

        def apart(eng):
            eng.sem_inc(waited, 1)

        class Phase:

            def __init__(self, eng):
                self.eng, self.k, self.img = eng, 0, None

            def image(self, img):
                self.k, self.img = 0, img

            def end(self):
                self.k += 1
                apart(self.eng)
                self.eng.drain().then_inc(phase_done, 1)
                if self.img is None:
                    self.eng.wait_ge(phase_done, ENGINES * self.k)
                else:
                    self.eng.wait_ge(phase_done, self.img * (ENGINES * PHASES) + ENGINES * (self.k + 1))

        class Own:

            def __init__(self, eng, s, per, pro):
                self.eng, self.s, self.per, self.pro, self.n, self.img = eng, s, per, pro, 0, None

            def image(self, img):
                assert self.n == self.pro, self.n
                self.img = img

            def __call__(self, ins):
                ins.then_inc(self.s, 1)
                self.n += 1
                self.eng.wait_ge(self.s, self.n if self.img is None else self.img * self.per + self.n)

        def skewed(eng, unroll, ops):
            lo, hi = min(s for s, _ in ops), max(s for s, _ in ops)
            start = -(-(4 - lo) // unroll) * unroll
            stop = (NC - hi) // unroll * unroll

            def step(t, k):
                for s, op in ops:
                    if not isinstance(t, int) or 0 <= t + s < NC:
                        op(t + s, k + s)
            for t in range(-hi, start):
                step(t, t)
            with eng.Fori(start, stop - unroll + 1, unroll) as i:
                for j in range(unroll):
                    step(i + j, j)
            for t in range(stop, NC - lo):
                step(t, t)

        def reuse(eng, s, first, c, ring):
            if not isinstance(c, int) or c >= ring:
                eng.wait_ge(s, first + (c - (ring - 1)))

        def ident(n):
            return K["ident"][0:n, 0:n]

        def jobs(first, count, mine, read):
            for j in range(count):
                if (first + j) % 2 == mine:
                    read(first + j, j, bank[2 + (first + j) % 3])

        def up_columns(mine, evacuate):
            def read(n, j, b):
                k = min(PERBANK, C - j * PERBANK)
                evacuate(n, sta3[:, j * PERBANK:j * PERBANK + k, :], b[0:W, 0:k * GRID].rearrange("p (c h) -> p c h", c=k))
            jobs(0, NJOB, mine, read)

        def up_rows(mine, evacuate):
            def read(n, j, b):
                k = min(PERBANK, GRID - j * PERBANK)
                evacuate(n, xu3[:, j * PERBANK:j * PERBANK + k, :], b[0:C, 0:k * GRID].rearrange("p (h w) -> p h w", h=k))
            jobs(NJOB, NJOB, mine, read)

        def down_rows(mine, evacuate):
            def read(n, j, b):
                evacuate(n, y13[:, 8 * j:8 * j + 8, :], b[0:GRID, 0:8 * W].rearrange("p (c w) -> p c w", c=8))
            jobs(2 * NJOB, 12, mine, read)

        def down_columns(img, dve, v):
            for j in range(8):
                n = 2 * NJOB + 12 + j
                dve.wait_ge(job_ready, img * JOBS + (n + 1))
                dst = xT3[:, :, 8 * j:8 * j + 8].rearrange("p h w -> p w h")
                v.scalar_tensor_tensor(dst, bank[2 + n % 3][0:C, :].rearrange("p (w h) -> p w h", w=8), out0i[0:C, 0:1], dst,
                                       ALU.add, ALU.add).then_inc(job_add, 1)

        block = ctx.enter_context(nc.Block())

        @block.sync
        def _(sp):
            n = [0]

            def load(dst, src):
                sp.dma_start(dst, src).then_inc(loads, 16)
                n[0] += 1

            load(cst[:, :], a["consts"])
            load(w1n, a["W1"].rearrange("(k p) c -> p k c", p=128))
            load(w1t[0:C, :], a["W1T"])
            load(w2t, a["W2T"].rearrange("(k p) c -> p k c", p=128))
            load(coef, a["coef"].rearrange("(k p) c -> p k c", p=128))
            load(b1[:, :], a["b1"])
            load(b2[0:C, :], a["b2"])
            load(win[0:C, :], a["w_in"])
            load(wconv[0:C], a["w_conv"].rearrange("(g p) t -> p g t", g=HALF))
            load(bconv[0:C, :], a["b_conv"])
            load(dsk[0:C], a["Ds"].rearrange("(g p) k -> p g k", g=HALF))
            load(lng[0:C, :], a["ln_g"])
            load(lnb[0:C, :], a["ln_b"])
            load(wout[0:C], a["w_out"].rearrange("(g p) c -> p g c", g=HALF))
            for o in range(2):
                for d in range(2):
                    k = o + 2 * d
                    load(wtok[0:C, o, d], a["wtok"][o, d].rearrange("(g p) n -> p g n", g=HALF))
                    load(dtb[Q * d:Q * d + Q, o, :], a["dt_bias"][k:k + 1, :].broadcast_to((Q, R)))
                    load(aneg[Q * d:Q * d + Q, o, :], a["A_logs"][k:k + 1, :].broadcast_to((Q, R)))
            assert n[0] == NLOAD, n
            sp.sem_inc(u_free, 1)
            sp.sem_inc(stored, 16)
            with sp.Fori(0, images) as img:
                sp.wait_ge(u_free, img + 1)
                sp.dma_start(xs3, a["x"][bass.ds(img, 1)].rearrange("b h w c -> (b h) w c")).then_inc(x_in, 16)
                sp.wait_ge(fin_done, img * NBLK + NBLK)
                sp.dma_start(out[bass.ds(img, 1)].rearrange("b h w c -> (b h w) c").rearrange("(n p) c -> p n c", p=128),
                             ot.rearrange("p (n c) -> p n c", c=C)).then_inc(stored, 16)
            sp.wait_ge(stored, 16 * images + 16)

        @block.tensor
        def _(pe):
            mm = nc.tensor.matmul
            ph = Phase(pe)
            pe.wait_ge(loads, 16 * NLOAD)
            pe.wait_ge(w2_scaled, 1)
            for k in range(KH):
                mm(bank[0][0:C, 0:C], w1n[:, k, :], w2l[:, k, :], start=(k == 0), stop=(k == KH - 1))
            for k in range(KH):
                mm(bank[1][0:C, 0:1], w2t[:, k, :], vconst[:, k:k + 1], start=(k == 0), stop=(k == KH - 1))
            for g in range(HALF):
                mm(bank[2][0:C, 0:C], K["mean192"][0:C, :], woutc[0:C, g, 0:C], start=(g == 0), stop=(g == 1))
            for g in range(HALF):
                i = mm(bank[3][0:1, 0:C], lnb[0:C, g:g + 1], wout[0:C, g, :], start=(g == 0), stop=(g == 1))
            i.then_inc(folded, 1)
            ph.end()
            with pe.Fori(0, images) as img:
                ph.image(img)
                pe.wait_ge(x_in, img * 16 + 16)
                for j in range(8):
                    if j >= 2:
                        pe.wait_ge(tr_read, img * 8 + (j - 1))
                    apart(pe)
                    for k in range(8):
                        i = nc.tensor.transpose(bank[j % 2][0:C, k * H:(k + 1) * H], xs3[:, 8 * j + k, :], ident(H))
                    i.then_inc(tr_ready, 1)
                job = [0]

                def drained(n):
                    if n >= JOBS - 8:
                        pe.wait_ge(job_add, img * 8 + (n - (JOBS - 8) + 1))
                    else:
                        pe.wait_ge(job_act if n % 2 == 0 else job_dve, img * ((JOBS - 8) // 2) + (n // 2 + 1))

                def resample(count, per_bank, product):
                    for j in range(-(-count // per_bank)):
                        n = job[0]
                        if n >= 3:
                            drained(n - 3)
                            apart(pe)
                        for k in range(j * per_bank, min(count, (j + 1) * per_bank)):
                            i = product(bank[2 + n % 3], k - j * per_bank, k)
                        i.then_inc(job_ready, 1)
                        job[0] += 1

                def all_drained():
                    for n in range(job[0] - 2, job[0]):
                        drained(n)

                def norm(k, shift):
                    pe.wait_ge(mom_ready, img * 2 + (k + 1))
                    mm(bank[0][0:C, 0:2], K["group"][0:C, :], mom[0:C, :], start=True, stop=True).then_inc(grp_ready, 1)
                    pe.wait_ge(nmr_ready, img * 2 + (k + 1))
                    shift().then_inc(shift_ready, 1)

                def shift_hidden():
                    for k in range(KH):
                        mm(bank[1][:, k:k + 1], w1t[0:C, 128 * k:128 * k + 128], nmr[0:C, :], start=True, stop=True)
                    return mm(bank[1][0:C, KH:KH + 1], lin[0:C, :], nmr[0:C, :], start=True, stop=True)

                def shift_in():
                    for g in range(HALF):
                        i = mm(bank[1][0:C, g:g + 1], win[0:C, C * g:C * g + C], nmr[0:C, :], start=True, stop=True)
                    return i

                resample(C, PERBANK, lambda b, k, c: mm(
                    b[0:W, k * GRID:(k + 1) * GRID], xs3[:, :, c], K["up"][0:H, :], start=True, stop=True))
                all_drained()
                norm(0, shift_hidden)
                apart(pe)
                resample(GRID, PERBANK, lambda b, k, h: mm(
                    b[0:C, k * GRID:(k + 1) * GRID], sta3[:, :, h], K["up"][0:W, :], start=True, stop=True))
                all_drained()
                ph.end()

                def hidden(t):
                    if t >= 2:
                        pe.wait_ge(hid_sq, img * (NTILE * KH) + KH * (t - 1))
                    for k in range(KH):
                        mm(bank[3 * (t % 2) + k][:, 0:NROW * GRID], w1s[0:C, 128 * k:128 * k + 128],
                           xu3[:, NROW * t:NROW * (t + 1), :], start=True, stop=True).then_inc(hid_ready, 1)

                def project(t):
                    pe.wait_ge(hid_sq, img * (NTILE * KH) + KH * (t + 1))
                    if t >= 2:
                        pe.wait_ge(proj_read, img * NTILE + (t - 1))
                    for h in range(NROW):
                        o = bank[6 + t % 2][0:GRID, h * C:(h + 1) * C]
                        mm(o, xu3[:, NROW * t + h, :], lins[0:C, :], start=True, stop=False)
                        for k in range(KH):
                            i = mm(o, sq[:, t % 2, k, h * GRID:(h + 1) * GRID], w2s[:, k, :], start=False, stop=(k == KH - 1))
                    i.then_inc(proj_ready, 1)

                for t in range(NTILE):
                    hidden(t)
                    if t:
                        project(t - 1)
                project(NTILE - 1)
                ph.end()
                resample(C, 8, lambda b, k, c: mm(
                    b[0:GRID, k * W:(k + 1) * W], z3[:, :, c], K["down"][0:GRID, :], start=True, stop=True))
                all_drained()
                resample(W, 8, lambda b, k, w: mm(
                    b[0:C, k * H:(k + 1) * H], y13[:, :, w], K["down"][0:GRID, :], start=True, stop=True))
                assert job[0] == JOBS
                norm(1, shift_in)
                ph.end()
                for j in range(16):
                    g, k = divmod(j, 8)
                    if j >= 4:
                        pe.wait_ge(in_read, img * 16 + (j - 3))
                    mm(bank[j % 4][0:C, :], wins[0:C, C * g:C * g + C], xT[0:C, 512 * k:512 * k + 512],
                       start=True, stop=True).then_inc(in_ready, 1)
                ph.end()
                ph.end()

                for o in range(2):
                    n0 = img * (2 * NC) + o * NC
                    m0 = img * (6 * NC) + o * 3 * NC
                    v0 = img * (4 * NC) + o * 2 * NC

                    def tokens(c, s):
                        pe.wait_ge(uc_ready, m0 + (c + 1))
                        reuse(pe, tok_out, n0, c, 2)
                        for d in range(2):
                            for g in range(HALF):
                                i = mm(bank[s % 2][Q * d:Q * d + Q, 0:NT], uc[0:C, s % 2, g, :], wtok[0:C, o, d, g, :],
                                       start=(g == 0), stop=(g == HALF - 1))
                        i.then_inc(tok_ready, 1)

                    def turn(c, s):
                        pe.wait_ge(tok_out, n0 + (c + 1))
                        reuse(pe, bct_in, n0, c, 2)
                        b = bank[2 + s % 2]
                        mm(b[0:2 * N, 0:2 * Q], tk[:, s % 2, R:R + 2 * N], K["ident"], start=True, stop=True)
                        mm(b[0:2 * N, 2 * Q:3 * Q], tk[:, s % 2, R + 2 * N:NT], K["fold"],
                           start=True, stop=True).then_inc(bct_ready, 1)

                    def cb(c, s):
                        pe.wait_ge(bct_in, n0 + (c + 1))
                        reuse(pe, g_read, n0, c, 2)
                        mm(bank[4 + s % 2][:, 0:Q], bct[0:2 * N, s % 2, 0:2 * Q], bct[0:2 * N, s % 2, 2 * Q:3 * Q],
                           start=True, stop=True).then_inc(g_ready, 1)

                    skewed(pe, 2, [(0, tokens), (-1, turn), (-2, cb)])
                    ph.end()
                    pe.wait_ge(aa_ready, img * 2 + (o + 1))
                    mm(bank[0][:, 0:NC * R], K["after"], aa[:, :], start=True, stop=True)
                    mm(bank[1][:, 0:NC * R], K["upto"], aa[:, :], start=True, stop=True)
                    mm(bank[2][0:C, 0:NC * R], K["dirsum"], aa[:, :], start=True, stop=True).then_inc(cum_ready, 1)
                    ph.end()

                    def turn_u(base):
                        def op(c, s):
                            pe.wait_ge(uc_ready, m0 + (base * NC + c + 1))
                            reuse(pe, up_ready, v0 + (base - 1) * NC, c, 2)
                            for d in range(2):
                                for g in range(HALF):
                                    i = mm(bank[s % 2][Q * d:Q * d + Q, g * C:(g + 1) * C], uc[0:C, s % 2, g, :], ident(C),
                                           start=True, stop=True)
                            i.then_inc(ut_ready, 1)
                        return op

                    def add_state(c, s):
                        pe.wait_ge(up_ready, v0 + (c + 1))
                        pe.wait_ge(bh_ready, n0 + (c + 1))
                        reuse(pe, dh_read, n0, c, 2)
                        for g in range(HALF):
                            for r in range(RH):
                                h = g * RH + r
                                i = mm(bank[2 + s % 2][32 * r:32 * r + 32, g * DH:(g + 1) * DH], bh[:, s % 2, h, :],
                                       up[:, s % 4, h * DH:(h + 1) * DH], start=True, stop=True)
                        i.then_inc(dh_ready, 1)

                    skewed(pe, 4, [(0, turn_u(1)), (-1, add_state)])
                    ph.end()
                    ph.end()

                    def log_decay(c, s):
                        pe.wait_ge(r_ready, n0 + (c + 1))
                        reuse(pe, e_ready, n0, c, 2)
                        mm(bank[2 + s % 2][:, 0:R * Q], K["after"], rr[:, s % 2, :], start=True, stop=True).then_inc(d_ready, 1)

                    def turn_c(c, s):
                        pe.wait_ge(ct_ready, n0 + (c + 1))
                        reuse(pe, ch_ready, n0, c, 2)
                        for g in range(HALF):
                            i = mm(bank[4 + s % 2][0:C, g * Q:(g + 1) * Q],
                                   ct[:, s % 2, RH * g:RH * g + RH, :].rearrange("p r n -> p (r n)"), K["fold"],
                                   start=True, stop=True)
                        i.then_inc(c_ready, 1)

                    def outputs(c, s):
                        pe.wait_ge(hbd_ready, n0 + (c + 1))
                        pe.wait_ge(ch_ready, n0 + (c + 1))
                        pe.wait_ge(m_ready, n0 + (c + 1))
                        reuse(pe, y_added, n0, c, 2)
                        b = bank[6 + s % 2]
                        for g in range(HALF):
                            mm(b[0:C, g * Q:(g + 1) * Q], hbd[0:C, s % 4, g, :], ch[0:C, s % 4, g, :], start=True, stop=True)
                            for r in range(RH):
                                h = g * RH + r
                                i = mm(b[32 * r:32 * r + 32, g * Q:(g + 1) * Q], up[:, s % 4, h * DH:(h + 1) * DH],
                                       mk[:, s % 2, h * Q:(h + 1) * Q], start=False, stop=True, skip_group_check=True)
                        i.then_inc(yc_ready, 1)

                    skewed(pe, 4, [(0, turn_u(2)), (0, log_decay), (0, turn_c), (-2, outputs)])
                    ph.end()
                for q in range(NG):
                    if q >= 2:
                        pe.wait_ge(fin_done, img * NBLK + GBLK * (q - 1))
                    pe.wait_ge(sq_ready, img * NG + (q + 1))
                    b, bx = bank[q % 2], bank[2 + q % 2]
                    for k in range(GBLK):
                        t0 = 128 * (GBLK * q + k)
                        for g in range(HALF):
                            mm(b[:, k * (C + 1):(k + 1) * (C + 1)], y[0:C, g * L + t0:g * L + t0 + 128],
                               woutc[0:C, g, :], start=(g == 0), stop=(g == 1))
                        for g in range(HALF):
                            mm(b[:, GBLK * (C + 1) + k:GBLK * (C + 1) + k + 1], ysq[0:C, g * L + t0:g * L + t0 + 128],
                               K["col192"][0:C, :], start=(g == 0), stop=(g == 1))
                        mm(bx[:, k * C:(k + 1) * C], xT[0:C, t0:t0 + 128], ident(C), start=True, stop=False)
                        i = mm(bx[:, k * C:(k + 1) * C], K["ones"][0:1, :], brow[0:1, :], start=False, stop=True)
                    i.then_inc(fin_ready, 1)
                ph.end()
                assert ph.k == PHASES, ph.k

        @block.scalar
        def _(act):
            ac = nc.scalar.activation
            ph = Phase(act)
            own = Own(act, act_own, 2, 0)
            act.wait_ge(loads, 16 * NLOAD)
            ac(aneg, aneg, ACT.Exp).then_inc(anegexp, 1)
            ph.end()
            with act.Fori(0, images) as img:
                ph.image(img)
                own.image(img)
                for j in range(8):
                    act.wait_ge(tr_ready, img * 8 + (j + 1))
                    ac(xT3[:, :, 8 * j:8 * j + 8].rearrange("p h w -> p w h"),
                       bank[j % 2][0:C, :].rearrange("p (w h) -> p w h", w=8), ACT.Copy).then_inc(tr_read, 1)

                def evacuate(n, dst, src):
                    act.wait_ge(job_ready, img * JOBS + (n + 1))
                    ac(dst, src, ACT.Copy).then_inc(job_act, 1)

                def norm(k):
                    act.wait_ge(var_ready, img * 2 + (k + 1))
                    own(ac(gvar[0:C, :], gvar[0:C, :], ACT.Ln))
                    ac(rstd[0:C, :], gvar[0:C, :], ACT.Exp, scale=-0.5).then_inc(rstd_ready, 1)

                up_columns(0, evacuate)
                norm(0)
                up_rows(0, evacuate)
                ph.end()
                for t in range(NTILE):
                    if t >= 2:
                        act.wait_ge(proj_ready, img * NTILE + (t - 1))
                    for k in range(KH):
                        act.wait_ge(hid_ready, img * (NTILE * KH) + (KH * t + k + 1))
                        ac(sq[:, t % 2, k, :], bank[3 * (t % 2) + k][:, 0:NROW * GRID], ACT.Square,
                           bias=bias1[:, k:k + 1]).then_inc(hid_sq, 1)
                ph.end()
                down_rows(0, evacuate)
                norm(1)
                ph.end()
                for j in range(16):
                    g, k = divmod(j, 8)
                    act.wait_ge(in_ready, img * 16 + (j + 1))
                    ac(xp4[:, g, 1 + 8 * k:9 + 8 * k, 1:1 + W], bank[j % 4][0:C, :].rearrange("p (h w) -> p h w", h=8),
                       ACT.Identity, bias=biasin[0:C, g:g + 1]).then_inc(in_read, 1)
                ph.end()
                for g in range(HALF):
                    act.wait_ge(conv_done, img * 2 + (g + 1))
                    ac(etmp[0:C, g * L:(g + 1) * L], u[0:C, g * L:(g + 1) * L], ACT.Exp, scale=-1.0).then_inc(exp_done, 1)
                ph.end()
                for g in range(HALF):
                    ac(y[0:C, g * L:(g + 1) * L], u[0:C, g * L:(g + 1) * L], ACT.Copy, scale=dsum[0:C, g:g + 1])
                for o in range(2):
                    n0 = img * (2 * NC) + o * NC
                    v0 = img * (4 * NC) + o * 2 * NC

                    def copy_u(read, first):
                        def op(c, s):
                            reuse(act, read, first, c, 2)
                            ac(uc[0:C, s % 2], chunk(u4, o, c), ACT.Copy).then_inc(uc_ready, 1)
                        return op

                    def token_out(c, s):
                        act.wait_ge(tok_ready, n0 + (c + 1))
                        reuse(act, bct_ready, n0, c, 2)
                        reuse(act, tok_kept, n0, c, 2)
                        ac(tk[:, s % 2, :], bank[s % 2][:, 0:NT], ACT.Copy).then_inc(tok_out, 1)

                    skewed(act, 2, [(1, copy_u(tok_ready, n0)), (0, token_out)])
                    ph.end()
                    act.wait_ge(abs_ready, img * 2 + (o + 1))
                    ac(expn[:, :], expn[:, :], ACT.Exp, scale=-1.0).then_inc(spe_ready, 1)
                    act.wait_ge(onep_ready, img * 2 + (o + 1))
                    ac(dt[:, :], onep[:, :], ACT.Ln).then_inc(ln_ready, 1)
                    act.wait_ge(cum_ready, img * 2 + (o + 1))
                    ac(tot[0:C, :], bank[2][0:C, 0:NC * R], ACT.Exp)
                    ac(wsuf[:, :], bank[0][:, 0:NC * R], ACT.Exp)
                    ac(ecum[:, :], bank[1][:, 0:NC * R], ACT.Exp).then_inc(cum_exp, 1)
                    ph.end()

                    def state_in(c, s):
                        act.wait_ge(dh_ready, n0 + (c + 1))
                        ac(states(hb)[:, :, one(c + 1)], bank[2 + s % 2][0:C, 0:HALF * DH].unsqueeze(2),
                           ACT.Copy).then_inc(dh_read, 1)

                    skewed(act, 4, [(1, copy_u(ut_ready, v0)), (-1, state_in)])
                    ph.end()
                    ph.end()

                    def decay(c, s):
                        act.wait_ge(d_ready, n0 + (c + 1))
                        reuse(act, m_ready, n0, c, 2)
                        ac(ee[:, s % 2, :], bank[2 + s % 2][:, 0:R * Q], ACT.Exp).then_inc(e_ready, 1)

                    def c_in(c, s):
                        act.wait_ge(c_ready, n0 + (c + 1))
                        reuse(act, yc_ready, n0, c, 4)
                        ac(ch[0:C, s % 4], bank[4 + s % 2][0:C, 0:HALF * Q].rearrange("p (g t) -> p g t", g=HALF),
                           ACT.Copy).then_inc(ch_ready, 1)

                    skewed(act, 4, [(1, copy_u(ut_ready, v0 + NC)), (0, decay), (0, c_in)])
                    ph.end()
                act.sem_inc(u_free, 1)
                part = L // NG
                for q in range(NG):
                    ac(ysq[0:C, :].rearrange("p (g t) -> p g t", g=HALF)[:, :, part * q:part * (q + 1)],
                       y[0:C, :].rearrange("p (g t) -> p g t", g=HALF)[:, :, part * q:part * (q + 1)],
                       ACT.Square).then_inc(sq_ready, 1)
                for q in range(NG):
                    act.wait_ge(fin_ready, img * NG + (q + 1))
                    if q >= 2:
                        act.wait_ge(fin_done, img * NBLK + GBLK * (q - 1))
                    ac(xsb[:, q % 2, :], bank[2 + q % 2][:, 0:GBLK * C], ACT.Copy).then_inc(fin_x, 1)
                    act.wait_ge(fin_var, img * NG + (q + 1))
                    ac(lns[:, q % 2, 2, :], lns[:, q % 2, 1, :], ACT.Ln).then_inc(fin_ln, 1)
                    act.wait_ge(fin_ln, img * NG + (q + 1))
                    ac(lns[:, q % 2, 3, :], lns[:, q % 2, 2, :], ACT.Exp, scale=-0.5).then_inc(fin_rstd, 1)
                ph.end()
                assert ph.k == PHASES and own.n == 2

        @block.gpsimd
        def _(pool):
            tt = nc.gpsimd.tensor_tensor
            ph = Phase(pool)
            ph.end()
            with pool.Fori(0, images) as img:
                ph.image(img)
                for _ in range(3):
                    ph.end()
                apart(pool)
                for g in range(HALF):
                    nc.gpsimd.memset(xp4[:, g, 0:PW:PW - 1, :], 0.0)
                    nc.gpsimd.memset(xp4[:, g, 1:PW - 1, 0:PW:PW - 1], 0.0)
                ph.end()
                ph.end()
                for o in range(2):
                    n0 = img * (2 * NC) + o * NC

                    def keep(c, s):
                        pool.wait_ge(tok_out, n0 + (c + 1))
                        apart(pool)
                        nc.gpsimd.tensor_copy(tok3[:, one(c), :], tk[:, s % 2, :].unsqueeze(1)).then_inc(tok_kept, 1)

                    skewed(pool, 2, [(0, keep)])
                    ph.end()
                    ph.end()

                    def weigh(dst, weight, col):
                        def op(c, s):
                            return tt(dst[:, s % 2], rc(weight)[:, one(c), :].rearrange("p c r -> p (c r)").unsqueeze(2)
                                      .broadcast_to((128, R, 2 * N)),
                                      tok3[:, one(c), col:col + 2 * N].broadcast_to((128, R, 2 * N)), ALU.mult)
                        return op

                    def weigh_b(c, s):
                        reuse(pool, dh_ready, n0, c, 2)
                        weigh(bh, wsuf, R)(c, s).then_inc(bh_ready, 1)

                    skewed(pool, 4, [(0, weigh_b)])
                    ph.end()
                    ph.end()

                    def spread_a(c, s):
                        reuse(pool, d_ready, n0, c, 2)
                        tt(rr[:, s % 2].rearrange("p (r t) -> p r t", r=R),
                           rc(aa)[:, one(c), :].rearrange("p c r -> p (c r)").unsqueeze(2).broadcast_to((128, R, Q)),
                           K["tri"].unsqueeze(1).broadcast_to((128, R, Q)), ALU.mult).then_inc(r_ready, 1)

                    def weigh_c(c, s):
                        reuse(pool, c_ready, n0, c, 2)
                        weigh(ct, ecum, R + 2 * N)(c, s).then_inc(ct_ready, 1)

                    def state_out(c, s):
                        reuse(pool, yc_ready, n0, c, 4)
                        for g in range(HALF):
                            i = tt(hbd[0:C, s % 4, g].rearrange("p (r d) -> p r d", r=RH),
                                   states(hf)[:, g * DH:(g + 1) * DH, one(c)].rearrange("p d c -> p c d")
                                   .broadcast_to((C, RH, DH)),
                                   K["headsel"][0:C, :].unsqueeze(2).broadcast_to((C, RH, DH)), ALU.mult)
                        i.then_inc(hbd_ready, 1)

                    skewed(pool, 4, [(0, spread_a), (0, weigh_c), (0, state_out)])
                    ph.end()
                ph.end()
                assert ph.k == PHASES

        @block.vector
        def _(dve):
            v = nc.vector
            ph = Phase(dve)
            PRO, PER = 6, 92
            own = Own(dve, dve_own, PER, PRO)
            dve.wait_ge(loads, 16 * NLOAD)
            for k in range(KH):
                v.tensor_scalar(w2s[:, k, :], w2t[:, k, :], coef[:, k, 2:3], None, ALU.mult)
                v.tensor_scalar(w2l[:, k, :], w2t[:, k, :], coef[:, k, 1:2], None, ALU.mult)
                v.scalar_tensor_tensor(vconst[:, k:k + 1], b1[:, k:k + 1], coef[:, k, 1:2], coef[:, k, 0:1], ALU.mult, ALU.add)
            for g in range(HALF):
                v.tensor_scalar(woutc[0:C, g, 0:C], wout[0:C, g, :], lng[0:C, g:g + 1], None, ALU.mult)
            v.memset(woutc[0:C, :, C:C + 1], 1.0 / DI).then_inc(w2_scaled, 1)
            v.tensor_reduce(dsum[0:C, :], dsk[0:C], mybir.AxisListType.X, ALU.add)
            dve.wait_ge(anegexp, 1)
            own(v.tensor_scalar(aneg, aneg, -1.0, None, ALU.mult))
            dve.wait_ge(folded, 1)
            own(v.tensor_copy(lin[0:C, :], bank[0][0:C, 0:C]))
            own(v.tensor_tensor(out0[0:C, :], bank[1][0:C, 0:1], b2[0:C, :], ALU.add))
            for g in range(HALF):
                own(v.tensor_tensor(woutc[0:C, g, 0:C], woutc[0:C, g, 0:C], bank[2][0:C, 0:C], ALU.subtract))
            own(v.tensor_copy(brow[0:1, :], bank[3][0:1, 0:C]))
            ph.end()
            with dve.Fori(0, images) as img:
                ph.image(img)
                own.image(img)

                def evacuate(n, dst, src):
                    dve.wait_ge(job_ready, img * JOBS + (n + 1))
                    v.tensor_copy(dst, src).then_inc(job_dve, 1)

                def norm(k):
                    for j in range(8):
                        i = v.bn_stats(bn[0:C, j, :], xT[0:C, 512 * j:512 * j + 512])
                    own(i)
                    apart(dve)
                    own(v.bn_aggr(mv[0:C, :], bn[0:C]))
                    v.tensor_copy(mom[0:C, 0:1], mv[0:C, 0:1])
                    v.scalar_tensor_tensor(mom[0:C, 1:2], mv[0:C, 0:1], mv[0:C, 0:1], mv[0:C, 1:2],
                                           ALU.mult, ALU.add).then_inc(mom_ready, 1)
                    dve.wait_ge(grp_ready, img * 2 + (k + 1))
                    own(v.tensor_copy(gst[0:C, :], bank[0][0:C, 0:2]))
                    own(v.tensor_tensor(gsq[0:C, :], gst[0:C, 0:1], gst[0:C, 0:1], ALU.mult))
                    own(v.tensor_tensor(gvar[0:C, :], gst[0:C, 1:2], gsq[0:C, :], ALU.subtract))
                    v.tensor_scalar(gvar[0:C, :], gvar[0:C, :], 0.0, 1e-5, ALU.max, ALU.add).then_inc(var_ready, 1)
                    dve.wait_ge(rstd_ready, img * 2 + (k + 1))
                    v.scalar_tensor_tensor(nmr[0:C, :], gst[0:C, 0:1], -1.0, rstd[0:C, :],
                                           ALU.mult, ALU.mult).then_inc(nmr_ready, 1)

                up_columns(1, evacuate)
                dve.wait_ge(tr_read, img * 8 + 8)
                norm(0)
                v.tensor_scalar(w1s[0:C, :], w1t[0:C, :], rstd[0:C, 0:1], None, ALU.mult)
                v.tensor_scalar(lins[0:C, :], lin[0:C, :], rstd[0:C, 0:1], None, ALU.mult)
                dve.wait_ge(shift_ready, img * 2 + 1)
                v.tensor_tensor(bias1[:, :], bank[1][:, 0:KH], b1[:, :], ALU.add)
                v.tensor_tensor(out0i[0:C, :], bank[1][0:C, KH:KH + 1], out0[0:C, :], ALU.add)
                up_rows(1, evacuate)
                ph.end()
                for t in range(NTILE):
                    dve.wait_ge(proj_ready, img * NTILE + (t + 1))
                    v.tensor_copy(z3[:, NROW * t:NROW * (t + 1), :],
                                  bank[6 + t % 2][0:GRID, 0:NROW * C].rearrange("p (h c) -> p h c", h=NROW)).then_inc(proj_read, 1)
                ph.end()
                down_rows(1, evacuate)
                down_columns(img, dve, v)
                dve.wait_ge(job_add, img * 8 + 8)
                norm(1)
                own(v.tensor_scalar(wins[0:C, :], win[0:C, :], rstd[0:C, 0:1], None, ALU.mult))
                dve.wait_ge(shift_ready, img * 2 + 2)
                own(v.tensor_copy(biasin[0:C, :], bank[1][0:C, 0:HALF]))
                ph.end()
                ph.end()
                for g in range(HALF):
                    for t in range(9):
                        src = xp4[:, g, t // 3:t // 3 + H, t % 3:t % 3 + W]
                        dst = u4[:, g]
                        if t == 0:
                            own(v.tensor_scalar(dst, src, wconv[0:C, g, 0:1], bconv[0:C, g:g + 1], ALU.mult, ALU.add))
                        else:
                            i = v.scalar_tensor_tensor(dst, src, wconv[0:C, g, t:t + 1], dst, ALU.mult, ALU.add)
                            if t < 8:
                                own(i)
                            else:
                                i.then_inc(conv_done, 1)
                for g in range(HALF):
                    dve.wait_ge(exp_done, img * 2 + (g + 1))
                    e_, u_ = etmp[0:C, g * L:(g + 1) * L], u[0:C, g * L:(g + 1) * L]
                    own(v.tensor_scalar(e_, e_, 1.0, None, ALU.add))
                    own(v.reciprocal(e_, e_))
                    own(v.tensor_tensor(u_, u_, e_, ALU.mult))
                ph.end()
                dve.wait_ge(stored, img * 16 + 16)
                for o in range(2):
                    n0 = img * (2 * NC) + o * NC
                    v0 = img * (4 * NC) + o * 2 * NC

                    def copy_bc(c, s):
                        dve.wait_ge(bct_ready, n0 + (c + 1))
                        reuse(dve, g_ready, n0, c, 2)
                        v.tensor_copy(bct[0:2 * N, s % 2, :], bank[2 + s % 2][0:2 * N, 0:3 * Q]).then_inc(bct_in, 1)

                    def mask_g(c, s):
                        dve.wait_ge(g_ready, n0 + (c + 1))
                        v.tensor_tensor(gm3[:, one(c), :], bank[4 + s % 2][:, 0:Q].unsqueeze(1), K["tri"].unsqueeze(1),
                                        ALU.mult).then_inc(g_read, 1)

                    skewed(dve, 2, [(-1, copy_bc), (-2, mask_g)])
                    ph.end()
                    own(v.tensor_tensor(rc(dtraw), tok3[:, :, 0:R], dtb[:, o, :].unsqueeze(1).broadcast_to((128, NC, R)), ALU.add))
                    v.scalar_tensor_tensor(expn[:, :], dtraw[:, :], -1.0, dtraw[:, :], ALU.mult, ALU.max).then_inc(abs_ready, 1)
                    dve.wait_ge(spe_ready, img * 2 + (o + 1))
                    v.tensor_scalar(onep[:, :], expn[:, :], 1.0, None, ALU.add).then_inc(onep_ready, 1)
                    dve.wait_ge(onep_ready, img * 2 + (o + 1))
                    own(v.tensor_scalar(den[:, :], onep[:, :], -1.0, None, ALU.add))
                    own(v.tensor_scalar(tiny[:, :], den[:, :], 0.0, None, ALU.is_equal))
                    own(v.tensor_tensor(den[:, :], den[:, :], tiny[:, :], ALU.add))
                    own(v.reciprocal(den[:, :], den[:, :]))
                    own(v.tensor_tensor(den[:, :], den[:, :], expn[:, :], ALU.mult))
                    own(v.tensor_tensor(tiny[:, :], tiny[:, :], expn[:, :], ALU.mult))
                    dve.wait_ge(ln_ready, img * 2 + (o + 1))
                    own(v.tensor_tensor(dt[:, :], dt[:, :], den[:, :], ALU.mult))
                    own(v.tensor_tensor(dt[:, :], dt[:, :], tiny[:, :], ALU.add))
                    own(v.scalar_tensor_tensor(dt[:, :], dtraw[:, :], 0.0, dt[:, :], ALU.max, ALU.add))
                    v.tensor_tensor(rc(aa), rc(dt), aneg[:, o, :].unsqueeze(1).broadcast_to((128, NC, R)),
                                    ALU.mult).then_inc(aa_ready, 1)
                    dve.wait_ge(cum_exp, img * 2 + (o + 1))
                    own(v.tensor_tensor(tot[0:C, :].rearrange("p (n r) -> p n r", r=RH), tot[0:C, :].rearrange("p (n r) -> p n r", r=RH),
                                        K["headsel"][0:C, :].unsqueeze(1).broadcast_to((C, HALF * NC, RH)), ALU.mult))
                    own(v.tensor_reduce(dec[0:C, :], tot[0:C, :].rearrange("p (n r) -> p n r", r=RH), mybir.AxisListType.X, ALU.add))
                    ph.end()

                    def scale_u(phase):
                        def op(c, s):
                            dve.wait_ge(ut_ready, v0 + (phase * NC + c + 1))
                            reuse(dve, dh_ready if phase == 0 else yc_ready, n0, c, 4)
                            v.tensor_tensor(up[:, s % 4].rearrange("p (r d) -> p r d", r=R),
                                            bank[s % 2][:, 0:R * DH].rearrange("p (r d) -> p r d", r=R),
                                            rc(dt)[:, one(c), :].rearrange("p c r -> p (c r)").unsqueeze(2).broadcast_to((128, R, DH)),
                                            ALU.mult).then_inc(up_ready, 1)
                        return op

                    skewed(dve, 4, [(0, scale_u(0))])
                    own(v.memset(decx[0:C, :], 0.0))
                    v.memset(states(hb)[:, :, 0:1], 0.0)
                    v.memset(hb[0:C, NST - 1:NST], 0.0)
                    dec3 = dec[0:C, :].rearrange("p (c g) -> p g c", g=HALF)
                    for g in range(HALF):
                        v.tensor_copy(states(decx)[:, g * DH:(g + 1) * DH, 1:SLOT],
                                      dec3[:, g:g + 1, :].broadcast_to((C, DH, NC)))
                    ph.end()
                    own(v.tensor_tensor_scan(hf[0:C, :], decx[0:C, :], hb[0:C, :], 0.0, ALU.mult, ALU.add))
                    own(v.tensor_tensor_scan(hb[0:C, ::-1], decx[0:C, ::-1], hb[0:C, ::-1], 0.0, ALU.mult, ALU.add))
                    own(v.tensor_scalar(hf[0:C, 0:NST - 2], hf[0:C, 0:NST - 2], K["fwd"][0:C, :], None, ALU.mult))
                    own(v.scalar_tensor_tensor(hf[0:C, 0:NST - 2], hb[0:C, 2:NST], K["bwd"][0:C, :], hf[0:C, 0:NST - 2],
                                               ALU.mult, ALU.add))
                    ph.end()

                    def weigh_g(c, s):
                        dve.wait_ge(e_ready, n0 + (c + 1))
                        reuse(dve, yc_ready, n0, c, 2)
                        v.tensor_tensor(mk[:, s % 2].rearrange("p (r t) -> p r t", r=R), ee[:, s % 2].rearrange("p (r t) -> p r t", r=R),
                                        gm3[:, one(c), :].broadcast_to((128, R, Q)), ALU.mult).then_inc(m_ready, 1)

                    def add_y(c, s):
                        dve.wait_ge(yc_ready, n0 + (c + 1))
                        yy = chunk(y4, o, c)
                        v.tensor_tensor(yy, yy, bank[6 + s % 2][0:C, 0:HALF * Q].rearrange("p (g t) -> p g t", g=HALF),
                                        ALU.add).then_inc(y_added, 1)

                    skewed(dve, 4, [(0, scale_u(1)), (-1, weigh_g), (-3, add_y)])
                    ph.end()

                def statistics(q):
                    dve.wait_ge(fin_ready, img * NG + (q + 1))
                    b = bank[q % 2]
                    own(v.tensor_copy(lns[:, q % 2, 0, :], b[:, C:C + (GBLK - 1) * (C + 1) + 1:C + 1]))
                    own(v.tensor_tensor(lns[:, q % 2, 0, :], lns[:, q % 2, 0, :], lns[:, q % 2, 0, :], ALU.mult))
                    own(v.tensor_tensor(lns[:, q % 2, 1, :], b[:, GBLK * (C + 1):GBLK * (C + 1) + GBLK], lns[:, q % 2, 0, :], ALU.subtract))
                    v.tensor_scalar(lns[:, q % 2, 1, :], lns[:, q % 2, 1, :], 0.0, 1e-5, ALU.max, ALU.add).then_inc(fin_var, 1)

                def finish(q):
                    dve.wait_ge(fin_rstd, img * NG + (q + 1))
                    for k in range(GBLK):
                        n = GBLK * q + k
                        v.scalar_tensor_tensor(ot[:, n * C:(n + 1) * C], bank[q % 2][:, k * (C + 1):k * (C + 1) + C],
                                               lns[:, q % 2, 3, k:k + 1], xsb[:, q % 2, k * C:(k + 1) * C],
                                               ALU.mult, ALU.add).then_inc(fin_done, 1)

                for q in range(NG):
                    statistics(q)
                    if q:
                        finish(q - 1)
                finish(NG - 1)
                ph.end()
                assert ph.k == PHASES and own.n == PRO + PER, own.n

    return nc


def constants():
    import numpy as np

    theta = 2 * np.pi * (np.arange(GRID) + 0.25) / GRID
    pos = 2 * np.pi * np.arange(W) / W
    freq = np.arange(-W // 2, W // 2 + 1)
    phase = np.exp(1j * freq[:, None, None] * (theta[None, :, None] - pos[None, None, :]))
    edge = np.where(abs(freq) == W // 2, 0.5, 1.0)[:, None, None]
    col = {
        "up": (phase.sum(0).real / W).T,
        "down": (phase * edge).sum(0).real / GRID,
        "ident": np.eye(128),
        "fold": np.tile(np.eye(Q), (2, 1)),
    }
    j = np.arange(Q)
    two = np.zeros((2, Q, 2, Q))
    two[0, :, 0] = j[:, None] > j[None, :]
    two[1, :, 1] = j[:, None] < j[None, :]
    col["after"] = two.reshape(128, 128)
    two = np.zeros((2, Q, 2, Q))
    two[0, :, 0] = j[:, None] <= j[None, :]
    two[1, :, 1] = j[:, None] >= j[None, :]
    col["upto"] = two.reshape(128, 128)
    col["tri"] = np.concatenate([two[0, :, 0], two[1, :, 1]])
    p = np.arange(C)
    direction = p % (2 * N) // N
    col["dirsum"] = np.repeat(np.arange(2), Q)[:, None] == direction[None, :]
    col["group"] = (p[:, None] // GROUP == p[None, :] // GROUP) / GROUP
    col["headsel"] = p[:, None] // (2 * N) == np.arange(RH)[None, :]
    col["fwd"] = (direction == 0)[:, None]
    col["bwd"] = (direction == 1)[:, None]
    col["mean192"] = np.full((C, C), 1.0 / DI)
    col["ones"] = np.ones((1, 128))
    col["col192"] = np.full((C, 1), 1.0 / DI)
    out = np.zeros((128, CONST_N), np.float32)
    for name, v in col.items():
        s, e = CONST_AT[name]
        assert v.shape[1] == e - s, name
        out[:v.shape[0], s:e] = v
    return out


def laid_out(inputs):
    import numpy as np

    i = {k: np.asarray(v) for k, v in inputs.items()}
    xp = i["L1_conv_x_proj_weight"]
    wtok = np.zeros((2, 2, DI, NT), np.float32)
    for o in range(2):
        for d in range(2):
            w = xp[o + 2 * d].T
            wtok[o, d, :, 0:R] = w[:, 0:R]
            wtok[o, d, :, R + d * N:R + (d + 1) * N] = w[:, R:R + N]
            wtok[o, d, :, R + (2 + d) * N:R + (3 + d) * N] = w[:, R + N:R + 2 * N]

    def cols(v, p):
        return v.reshape(-1, p).T

    arrays = {
        "x": i["x"], "consts": constants(), "W1": i["L0_conv_W1"], "W1T": i["L0_conv_W1"].T, "W2T": i["L0_conv_W2"].T,
        "b1": cols(i["L0_conv_b1"], 128), "b2": cols(i["L0_conv_b2"], C), "coef": i["L0_conv_coef"], "w_in": i["L1_conv_w_in"],
        "w_conv": i["L1_conv_w_conv"].reshape(9, DI).T, "b_conv": cols(i["L1_conv_b_conv"], C), "wtok": wtok,
        "A_logs": i["L1_conv_A_logs"], "dt_bias": i["L1_conv_dt_bias"], "Ds": i["L1_conv_Ds"].reshape(4, DI).T,
        "ln_g": cols(i["L1_conv_ln_g"], C), "ln_b": cols(i["L1_conv_ln_b"], C), "w_out": i["L1_conv_w_out"],
    }
    return {f"in_{k}": np.ascontiguousarray(v) for k, v in arrays.items()}


def kernel(**inputs):
    import concourse.bacc as bacc
    from concourse.bass_utils import run_bass_kernel_spmd

    nc = bacc.Bacc("TRN2", target_bir_lowering=False, num_devices=1)
    arrays = laid_out(inputs)
    aps = {k[3:]: nc.dram_tensor(k, v.shape, mybir.dt.from_np(v.dtype), kind="ExternalInput").ap() for k, v in arrays.items()}
    out = nc.dram_tensor("out", (B, H, W, C), F32, kind="ExternalOutput").ap()
    build(nc, aps, out)
    r = run_bass_kernel_spmd(nc, [arrays], core_ids=[0])
    return r.results[0]["out"]
```

```python
from contextlib import ExitStack

import concourse.bass as bass
from concourse import mybir

F32 = mybir.dt.float32
F16 = mybir.dt.float16
ALU = mybir.AluOpType
ACT = mybir.ActivationFunctionType

B, H, W, C = 16, 64, 64, 96
L = H * W
GROUP = 3
HID = 4 * C
KH = HID // 128
GRID = 96
DI = 192
HALF = 2
R, DH, N = 6, 32, 16
RH = R // HALF
Q = 64
NC = L // Q
NT = R + 4 * N
SLOT = NC + 1
NST = HALF * DH * SLOT + 1
NROW = 4
NTILE = GRID // NROW
PERBANK = 5
NJOB = -(-C // PERBANK)
NBLK = L // 128
GBLK = 4
NG = NBLK // GBLK
PETAPS = (3, 4)
QUART = L // 4

CONST_PARTS = [("up", GRID), ("down", W), ("ident", 128), ("fold", Q), ("after", 128), ("upto", 128),
               ("dirsum", C), ("tri", Q), ("group", C), ("headsel", RH), ("fwd", 1), ("bwd", 1),
               ("mean192", C), ("col192", 1)]
CONST_AT, CONST_N = {}, 0
for _name, _n in CONST_PARTS:
    CONST_AT[_name] = (CONST_N, CONST_N + _n)
    CONST_N += _n


def build(nc, a, out, images=B, dump=None):
    ctx = ExitStack()
    with ctx:
        def sb(name, n, dt=F32):
            return ctx.enter_context(nc.sbuf_tensor(name, [128, n], dt))

        def sem(name):
            return ctx.enter_context(nc.semaphore(name))

        bank = [ctx.enter_context(nc.psum_tensor(f"bank{i}", [128, 512], F32)) for i in range(8)]

        cst = sb("cst", CONST_N)
        K = {k: cst[:, s:e] for k, (s, e) in CONST_AT.items()}
        w1n = sb("w1n", KH * C)[:, :].rearrange("p (k c) -> p k c", k=KH)
        w1t = sb("w1t", HID)
        w1s = sb("w1s", HID)
        w2t = sb("w2t", KH * C)[:, :].rearrange("p (k c) -> p k c", k=KH)
        w2s = sb("w2s", KH * C)[:, :].rearrange("p (k c) -> p k c", k=KH)
        w2l = sb("w2l", KH * C)[:, :].rearrange("p (k c) -> p k c", k=KH)
        lin = sb("lin", C)
        lins = sb("lins", C)
        coef = sb("coef", KH * 3)[:, :].rearrange("p (k c) -> p k c", k=KH)
        b1 = sb("b1", KH)
        vconst = sb("vconst", KH)
        b2 = sb("b2", 1)
        out0 = sb("out0", 1)
        win = sb("win", DI)
        wins = sb("wins", DI)
        wconv = sb("wconv", HALF * 9)[:, :].rearrange("p (g t) -> p g t", g=HALF)
        bconv = sb("bconv", HALF)
        diag = sb("diag", sum(PETAPS) * C)[:, :].rearrange("p (k c) -> p k c", c=C)
        wtok = sb("wtok", 2 * 2 * HALF * NT)[:, :].rearrange("p (o d g n) -> p o d g n", o=2, d=2, g=HALF)
        dtb = sb("dtb", 2 * R)[:, :].rearrange("p (o r) -> p o r", o=2)
        aneg = sb("aneg", 2 * R)[:, :].rearrange("p (o r) -> p o r", o=2)
        dsk = sb("dsk", HALF * 4)[:, :].rearrange("p (g k) -> p g k", g=HALF)
        dsum = sb("dsum", HALF)
        lng = sb("lng", HALF)
        lnb = sb("lnb", HALF)
        wout = sb("wout", HALF * C)[:, :].rearrange("p (g c) -> p g c", g=HALF)
        woutc = sb("woutc", HALF * C)[:, :].rearrange("p (g c) -> p g c", g=HALF)
        bcol = sb("bcol", 1)
        after16 = sb("after16", 128, F16)
        tri16 = sb("tri16", Q * R, F16)
        bn = sb("bn", 8 * 6)[:, :].rearrange("p (k s) -> p k s", s=6)
        mv = sb("mv", 2)
        mom = sb("mom", 2)
        gst = sb("gst", 2)
        gsq = sb("gsq", 1)
        gvar = sb("gvar", 1)
        rstd = sb("rstd", 1)
        nmr = sb("nmr", 1)
        bias1 = sb("bias1", KH)
        out0i = sb("out0i", 1)
        biasin = sb("biasin", HALF)
        dt = sb("dt", NC * R)
        aa = sb("aa", NC * R)
        ahi = sb("ahi", NC * R, F16)
        alo = sb("alo", NC * R, F16)
        r16 = sb("r16", 2 * 2 * Q * R, F16)[:, :].rearrange("p (s k n) -> p s k n", s=2, k=2)
        rstds = sb("rstds", 4 * NBLK)[:, :].rearrange("p (i n) -> p i n", i=4)
        wsuf = sb("wsuf", NC * R)
        ecum = sb("ecum", NC * R)
        tot = sb("tot", NC * R)
        dec = sb("dec", HALF * NC)
        xT = sb("xT", L)
        ARENA = 39491
        arena = sb("arena", ARENA)
        at = [0]

        def take(n, start=None):
            if start is not None:
                at[0] = start
            v = arena[:, at[0]:at[0] + n]
            at[0] += n
            assert at[0] <= ARENA, at
            return v

        xs = take(W * C, 0)
        y1 = xs
        st_a = take(GRID * C)
        z = st_a
        xu = take(GRID * GRID)
        sq = take(2 * KH * NROW * GRID).rearrange("p (s k n) -> p s k n", s=2, k=KH)
        PW = W + 2
        u = take(HALF * L, 0)
        y = take(HALF * L)
        etmp = y
        state_at = at[0]
        hf = take(NST)
        hb = take(NST)
        tokp = take(NC * NT)
        gm_at = at[0]
        xpad = take(HALF * PW * PW, state_at)
        ysq = take(HALF * L, state_at)
        gm = take(NC * Q, gm_at)
        ring_a1 = at[0]
        tk = take(4 * NT).rearrange("p (s n) -> p s n", s=4)
        bct = take(4 * 3 * Q).rearrange("p (s n) -> p s n", s=4)
        uc = take(4 * HALF * Q).rearrange("p (s g t) -> p s g t", s=4, g=HALF)
        dtraw, expn, onep, den, tiny, aclip = (take(NC * R, ring_a1 + k * NC * R) for k in range(6))
        ud = take(2 * HALF * 2 * Q, ring_a1).rearrange("p (s g k t) -> p s g k t", s=2, g=HALF, k=2)
        bh_at = at[0]
        bh = take(4 * R * 2 * N).rearrange("p (s r n) -> p s r n", s=4, r=R)
        ct = take(2 * R * 2 * N, bh_at).rearrange("p (s r n) -> p s r n", s=2, r=R)
        take(2 * R * 2 * N)
        up = take(4 * R * DH).rearrange("p (s n) -> p s n", s=4)
        ring_at = at[0]
        ee = take(2 * R * Q).rearrange("p (s n) -> p s n", s=2)
        mk = take(2 * R * Q).rearrange("p (s n) -> p s n", s=2)
        ch = take(4 * HALF * Q).rearrange("p (s g t) -> p s g t", s=4, g=HALF)
        hbd = take(4 * HALF * C).rearrange("p (s g n) -> p s g n", s=4, g=HALF)
        decx = take(NST, ring_at)
        xsb = take(3 * GBLK * C, ring_at).rearrange("p (s n) -> p s n", s=3)
        ot = take(NBLK * C, gm_at)

        xs3 = xs[0:H, :].rearrange("p (w c) -> p w c", w=W)
        sta3 = st_a[0:W, :].rearrange("p (c h) -> p c h", c=C)
        xu3 = xu[0:C, :].rearrange("p (h w) -> p h w", h=GRID)
        z3 = z[0:GRID, :].rearrange("p (h c) -> p h c", h=GRID)
        y13 = y1[0:GRID, :].rearrange("p (c w) -> p c w", c=C)
        xT3 = xT[0:C, :].rearrange("p (h w) -> p h w", h=H)
        u4 = u[0:C, :].rearrange("p (g h w) -> p g h w", g=HALF, h=H)
        y4 = y[0:C, :].rearrange("p (g h w) -> p g h w", g=HALF, h=H)
        xp4 = xpad[0:C, :].rearrange("p (g h w) -> p g h w", g=HALF, h=PW)
        tok3 = tokp.rearrange("p (c n) -> p c n", c=NC)
        gm3 = gm.rearrange("p (c t) -> p c t", c=NC)

        def rc(t):
            return t[:, :].rearrange("p (c r) -> p c r", c=NC)

        def states(t, shift=0):
            return t[0:C, shift:shift + HALF * DH * SLOT].rearrange("p (n c) -> p n c", c=SLOT)

        def one(c):
            return slice(c, c + 1) if isinstance(c, int) else bass.ds(c, 1)

        def chunk(t4, o, c):
            v = t4[:, :, one(c), :] if o == 0 else t4[:, :, :, one(c)]
            return v.rearrange("p g a b -> p g (a b)")

        loads, x_in, u_free, stored = sem("loads"), sem("x_in"), sem("u_free"), sem("stored")
        waited = sem("waited")
        phase_done = sem("phase_done")
        dve_own, act_own = sem("dve_own"), sem("act_own")
        w2_scaled, folded, anegexp = sem("w2_scaled"), sem("folded"), sem("anegexp")
        mom_ready, grp_ready, var_ready = sem("mom_ready"), sem("grp_ready"), sem("var_ready")
        rstd_ready, nmr_ready, shift_ready = sem("rstd_ready"), sem("nmr_ready"), sem("shift_ready")
        tr_ready, tr_read = sem("tr_ready"), sem("tr_read")
        job_ready, job_act, job_dve, job_add = sem("job_ready"), sem("job_act"), sem("job_dve"), sem("job_add")
        hid_ready, hid_sq, proj_ready, proj_read = sem("hid_ready"), sem("hid_sq"), sem("proj_ready"), sem("proj_read")
        in_ready, in_read, pads_ready = sem("in_ready"), sem("in_read"), sem("pads_ready")
        taps_ready, taps_read, conv_done, tanh_done = sem("taps_ready"), sem("taps_read"), sem("conv_done"), sem("tanh_done")
        abs_ready, spe_ready, onep_ready, ln_ready = sem("abs_ready"), sem("spe_ready"), sem("onep_ready"), sem("ln_ready")
        aa_ready, cum_ready, cum_exp = sem("aa_ready"), sem("cum_ready"), sem("cum_exp")
        uc_ready = sem("uc_ready")
        tok_ready, tok_out, tok_kept = sem("tok_ready"), sem("tok_out"), sem("tok_kept")
        bct_ready, bct_in, g_ready, g_read = sem("bct_ready"), sem("bct_in"), sem("g_ready"), sem("g_read")
        ut_ready, up_ready = sem("ut_ready"), sem("up_ready")
        bh_ready, dh_ready, dh_read = sem("bh_ready"), sem("dh_ready"), sem("dh_read")
        r_ready, d_ready, e_ready, m_ready = sem("r_ready"), sem("d_ready"), sem("e_ready"), sem("m_ready")
        ct_ready, c_ready, ch_ready = sem("ct_ready"), sem("c_ready"), sem("ch_ready")
        hbd_ready, yc_ready, y_added = sem("hbd_ready"), sem("yc_ready"), sem("y_added")
        stat_ready = sem("stat_ready")
        fin_ready, fin_x, fin_var, fin_ln, fin_rstd = (sem(n) for n in ("fin_ready", "fin_x", "fin_var", "fin_ln", "fin_rstd"))
        fin_done, sq_ready = sem("fin_done"), sem("sq_ready")

        ENGINES = 4
        PHASES = 15
        JOBS = 2 * NJOB + 12 + 8
        NLOAD = 26

        def apart(eng):
            eng.sem_inc(waited, 1)

        class Phase:

            def __init__(self, eng):
                self.eng, self.k, self.img = eng, 0, None

            def image(self, img):
                self.k, self.img = 0, img

            def end(self):
                self.k += 1
                apart(self.eng)
                self.eng.drain().then_inc(phase_done, 1)
                if self.img is None:
                    self.eng.wait_ge(phase_done, ENGINES * self.k)
                else:
                    self.eng.wait_ge(phase_done, self.img * (ENGINES * PHASES) + ENGINES * (self.k + 1))

        class Own:

            def __init__(self, eng, s, per, pro):
                self.eng, self.s, self.per, self.pro, self.n, self.img = eng, s, per, pro, 0, None

            def image(self, img):
                assert self.n == self.pro, self.n
                self.img = img

            def __call__(self, ins):
                ins.then_inc(self.s, 1)
                self.n += 1
                self.eng.wait_ge(self.s, self.n if self.img is None else self.img * self.per + self.n)

        def skewed(eng, unroll, ops):
            lo, hi = min(s for s, _ in ops), max(s for s, _ in ops)
            start = -(-(4 - lo) // unroll) * unroll
            stop = (NC - hi) // unroll * unroll

            def step(t, k):
                for s, op in ops:
                    if not isinstance(t, int) or 0 <= t + s < NC:
                        op(t + s, k + s)
            for t in range(-hi, start):
                step(t, t)
            with eng.Fori(start, stop - unroll + 1, unroll) as i:
                for j in range(unroll):
                    step(i + j, j)
            for t in range(stop, NC - lo):
                step(t, t)

        def reuse(eng, s, first, c, ring):
            if not isinstance(c, int) or c >= ring:
                eng.wait_ge(s, first + (c - (ring - 1)))

        def ident(n):
            return K["ident"][0:n, 0:n]

        def jobs(first, count, mine, read):
            for j in range(count):
                if (first + j) % 2 == mine:
                    read(first + j, j, bank[2 + (first + j) % 3])

        def up_columns(mine, evacuate):
            def read(n, j, b):
                k = min(PERBANK, C - j * PERBANK)
                evacuate(n, sta3[:, j * PERBANK:j * PERBANK + k, :], b[0:W, 0:k * GRID].rearrange("p (c h) -> p c h", c=k))
            jobs(0, NJOB, mine, read)

        def up_rows(mine, evacuate):
            def read(n, j, b):
                k = min(PERBANK, GRID - j * PERBANK)
                evacuate(n, xu3[:, j * PERBANK:j * PERBANK + k, :], b[0:C, 0:k * GRID].rearrange("p (h w) -> p h w", h=k))
            jobs(NJOB, NJOB, mine, read)

        def down_rows(mine, evacuate):
            def read(n, j, b):
                evacuate(n, y13[:, 8 * j:8 * j + 8, :], b[0:GRID, 0:8 * W].rearrange("p (c w) -> p c w", c=8))
            jobs(2 * NJOB, 12, mine, read)

        def down_columns(img, dve, v):
            for j in range(8):
                n = 2 * NJOB + 12 + j
                dve.wait_ge(job_ready, img * JOBS + (n + 1))
                dst = xT3[:, :, 8 * j:8 * j + 8].rearrange("p h w -> p w h")
                v.scalar_tensor_tensor(dst, bank[2 + n % 3][0:C, :].rearrange("p (w h) -> p w h", w=8), out0i[0:C, 0:1], dst,
                                       ALU.add, ALU.add).then_inc(job_add, 1)

        block = ctx.enter_context(nc.Block())

        @block.sync
        def _(sp):
            n = [0]

            def load(dst, src):
                sp.dma_start(dst, src).then_inc(loads, 16)
                n[0] += 1

            load(cst[:, :], a["consts"])
            load(w1n, a["W1"].rearrange("(k p) c -> p k c", p=128))
            load(w1t[0:C, :], a["W1T"])
            load(w2t, a["W2T"].rearrange("(k p) c -> p k c", p=128))
            load(coef, a["coef"].rearrange("(k p) c -> p k c", p=128))
            load(b1[:, :], a["b1"])
            load(b2[0:C, :], a["b2"])
            load(win[0:C, :], a["w_in"])
            load(wconv[0:C], a["w_conv"].rearrange("(g p) t -> p g t", g=HALF))
            load(bconv[0:C, :], a["b_conv"])
            load(dsk[0:C], a["Ds"].rearrange("(g p) k -> p g k", g=HALF))
            load(lng[0:C, :], a["ln_g"])
            load(lnb[0:C, :], a["ln_b"])
            load(wout[0:C], a["w_out"].rearrange("(g p) c -> p g c", g=HALF))
            for o in range(2):
                for d in range(2):
                    k = o + 2 * d
                    load(wtok[0:C, o, d], a["wtok"][o, d].rearrange("(g p) n -> p g n", g=HALF))
                    load(dtb[Q * d:Q * d + Q, o, :], a["dt_bias"][k:k + 1, :].broadcast_to((Q, R)))
                    load(aneg[Q * d:Q * d + Q, o, :], a["A_logs"][k:k + 1, :].broadcast_to((Q, R)))
            assert n[0] == NLOAD, n
            sp.sem_inc(u_free, 1)
            sp.sem_inc(stored, 16)
            with sp.Fori(0, images) as img:
                sp.wait_ge(u_free, img + 1)
                sp.dma_start(xs3, a["x"][bass.ds(img, 1)].rearrange("b h w c -> (b h) w c")).then_inc(x_in, 16)
                sp.wait_ge(fin_done, img * NBLK + NBLK)
                sp.dma_start(out[bass.ds(img, 1)].rearrange("b h w c -> (b h w) c").rearrange("(n p) c -> p n c", p=128),
                             ot.rearrange("p (n c) -> p n c", c=C)).then_inc(stored, 16)
            sp.wait_ge(stored, 16 * images + 16)

        @block.tensor
        def _(pe):
            mm = nc.tensor.matmul
            ph = Phase(pe)
            pe.wait_ge(loads, 16 * NLOAD)
            pe.wait_ge(w2_scaled, 1)
            for k in range(KH):
                mm(bank[0][0:C, 0:C], w1n[:, k, :], w2l[:, k, :], start=(k == 0), stop=(k == KH - 1))
            for k in range(KH):
                mm(bank[1][0:C, 0:1], w2t[:, k, :], vconst[:, k:k + 1], start=(k == 0), stop=(k == KH - 1))
            for g in range(HALF):
                mm(bank[2][0:C, 0:C], K["mean192"][0:C, :], woutc[0:C, g, :], start=(g == 0), stop=(g == 1))
            for g in range(HALF):
                i = mm(bank[3][0:C, 0:1], wout[0:C, g, :], lnb[0:C, g:g + 1], start=(g == 0), stop=(g == 1))
            i.then_inc(folded, 1)
            ph.end()
            with pe.Fori(0, images) as img:
                ph.image(img)
                pe.wait_ge(x_in, img * 16 + 16)
                for j in range(8):
                    if j >= 2:
                        pe.wait_ge(tr_read, img * 8 + (j - 1))
                    apart(pe)
                    for k in range(8):
                        i = nc.tensor.transpose(bank[j % 2][0:C, k * H:(k + 1) * H], xs3[:, 8 * j + k, :], ident(H))
                    i.then_inc(tr_ready, 1)
                job = [0]

                def drained(n):
                    if n >= JOBS - 8:
                        pe.wait_ge(job_add, img * 8 + (n - (JOBS - 8) + 1))
                    else:
                        pe.wait_ge(job_act if n % 2 == 0 else job_dve, img * ((JOBS - 8) // 2) + (n // 2 + 1))

                def resample(count, per_bank, product):
                    for j in range(-(-count // per_bank)):
                        n = job[0]
                        if n >= 3:
                            drained(n - 3)
                            apart(pe)
                        for k in range(j * per_bank, min(count, (j + 1) * per_bank)):
                            i = product(bank[2 + n % 3], k - j * per_bank, k)
                        i.then_inc(job_ready, 1)
                        job[0] += 1

                def all_drained():
                    for n in range(job[0] - 2, job[0]):
                        drained(n)

                def norm(k, shift):
                    pe.wait_ge(mom_ready, img * 2 + (k + 1))
                    mm(bank[0][0:C, 0:2], K["group"][0:C, :], mom[0:C, :], start=True, stop=True).then_inc(grp_ready, 1)
                    pe.wait_ge(nmr_ready, img * 2 + (k + 1))
                    shift().then_inc(shift_ready, 1)

                def shift_hidden():
                    for k in range(KH):
                        mm(bank[1][:, k:k + 1], w1t[0:C, 128 * k:128 * k + 128], nmr[0:C, :], start=True, stop=True)
                    return mm(bank[1][0:C, KH:KH + 1], lin[0:C, :], nmr[0:C, :], start=True, stop=True)

                def shift_in():
                    for g in range(HALF):
                        i = mm(bank[1][0:C, g:g + 1], win[0:C, C * g:C * g + C], nmr[0:C, :], start=True, stop=True)
                    return i

                resample(C, PERBANK, lambda b, k, c: mm(
                    b[0:W, k * GRID:(k + 1) * GRID], xs3[:, :, c], K["up"][0:H, :], start=True, stop=True))
                all_drained()
                norm(0, shift_hidden)
                apart(pe)
                resample(GRID, PERBANK, lambda b, k, h: mm(
                    b[0:C, k * GRID:(k + 1) * GRID], sta3[:, :, h], K["up"][0:W, :], start=True, stop=True))
                all_drained()
                ph.end()

                def hidden(t):
                    if t >= 2:
                        pe.wait_ge(hid_sq, img * (NTILE * KH) + KH * (t - 1))
                    for k in range(KH):
                        mm(bank[3 * (t % 2) + k][:, 0:NROW * GRID], w1s[0:C, 128 * k:128 * k + 128],
                           xu3[:, NROW * t:NROW * (t + 1), :], start=True, stop=True).then_inc(hid_ready, 1)

                def project(t):
                    pe.wait_ge(hid_sq, img * (NTILE * KH) + KH * (t + 1))
                    if t >= 2:
                        pe.wait_ge(proj_read, img * NTILE + (t - 1))
                    for h in range(NROW):
                        o = bank[6 + t % 2][0:GRID, h * C:(h + 1) * C]
                        mm(o, xu3[:, NROW * t + h, :], lins[0:C, :], start=True, stop=False)
                        for k in range(KH):
                            i = mm(o, sq[:, t % 2, k, h * GRID:(h + 1) * GRID], w2s[:, k, :], start=False, stop=(k == KH - 1))
                    i.then_inc(proj_ready, 1)

                for t in range(NTILE):
                    hidden(t)
                    if t:
                        project(t - 1)
                project(NTILE - 1)
                ph.end()
                resample(C, 8, lambda b, k, c: mm(
                    b[0:GRID, k * W:(k + 1) * W], z3[:, :, c], K["down"][0:GRID, :], start=True, stop=True))
                all_drained()
                resample(W, 8, lambda b, k, w: mm(
                    b[0:C, k * H:(k + 1) * H], y13[:, :, w], K["down"][0:GRID, :], start=True, stop=True))
                assert job[0] == JOBS
                norm(1, shift_in)
                ph.end()
                pe.wait_ge(pads_ready, img + 1)
                for g in range(HALF):
                    first, count = g * PETAPS[0], PETAPS[g]
                    for k in range(9):
                        if k < 8:
                            if 8 * g + k >= 4:
                                pe.wait_ge(in_read, img * 16 + (8 * g + k - 3))
                            mm(bank[k % 4][0:C, :], wins[0:C, C * g:C * g + C], xT[0:C, 512 * k:512 * k + 512],
                               start=True, stop=True).then_inc(in_ready, 1)
                        if k:
                            j = 8 * g + k - 1
                            pe.wait_ge(in_read, img * 16 + (8 * g + min(k + 1, 8)))
                            if j >= 4:
                                pe.wait_ge(taps_read, img * 16 + (j - 3))
                            for t in range(count):
                                i = mm(bank[4 + j % 4][0:C, :], diag[0:C, first + t, :],
                                       xp4[:, g, 8 * (k - 1) + t // 3:8 * k + t // 3, t % 3:t % 3 + W],
                                       start=(t == 0), stop=(t == count - 1))
                            i.then_inc(taps_ready, 1)
                ph.end()

                for o in range(2):
                    n0 = img * (2 * NC) + o * NC
                    m0 = img * (6 * NC) + o * 3 * NC
                    v0 = img * (4 * NC) + o * 2 * NC

                    def tokens(c, s):
                        pe.wait_ge(uc_ready, m0 + (c + 1))
                        reuse(pe, tok_out, n0, c, 2)
                        for d in range(2):
                            for g in range(HALF):
                                i = mm(bank[s % 2][Q * d:Q * d + Q, 0:NT], uc[0:C, s % 4, g, :], wtok[0:C, o, d, g, :],
                                       start=(g == 0), stop=(g == HALF - 1))
                        i.then_inc(tok_ready, 1)

                    def turn(c, s):
                        pe.wait_ge(tok_out, n0 + (c + 1))
                        reuse(pe, bct_in, n0, c, 2)
                        b = bank[2 + s % 2]
                        nc.tensor.transpose(b[0:2 * N, 0:2 * Q], tk[:, s % 4, R:R + 2 * N], K["ident"])
                        mm(b[0:2 * N, 2 * Q:3 * Q], tk[:, s % 4, R + 2 * N:NT], K["fold"],
                           start=True, stop=True).then_inc(bct_ready, 1)

                    def cb(c, s):
                        pe.wait_ge(bct_in, n0 + (c + 1))
                        reuse(pe, g_read, n0, c, 2)
                        mm(bank[4 + s % 2][:, 0:Q], bct[0:2 * N, s % 4, 0:2 * Q], bct[0:2 * N, s % 4, 2 * Q:3 * Q],
                           start=True, stop=True).then_inc(g_ready, 1)

                    skewed(pe, 4, [(0, tokens), (-2, turn), (-4, cb)])
                    ph.end()
                    pe.wait_ge(aa_ready, img * 2 + (o + 1))
                    mm(bank[0][:, 0:NC * R], K["after"], aa[:, :], start=True, stop=True)
                    mm(bank[1][:, 0:NC * R], K["upto"], aa[:, :], start=True, stop=True)
                    mm(bank[2][0:C, 0:NC * R], K["dirsum"], aa[:, :], start=True, stop=True).then_inc(cum_ready, 1)
                    ph.end()

                    def turn_u(base):
                        def op(c, s):
                            pe.wait_ge(uc_ready, m0 + (base * NC + c + 1))
                            reuse(pe, up_ready, v0 + (base - 1) * NC, c, 2)
                            apart(pe)
                            for g in range(HALF):
                                i = nc.tensor.transpose(bank[s % 2][:, g * C:(g + 1) * C],
                                                        ud[0:C, s % 2, g].rearrange("p k t -> p (k t)"), ident(C))
                            i.then_inc(ut_ready, 1)
                        return op

                    def add_state(c, s):
                        pe.wait_ge(up_ready, v0 + (c + 1))
                        pe.wait_ge(bh_ready, n0 + (c + 1))
                        reuse(pe, dh_read, n0, c, 2)
                        for g in range(HALF):
                            for r in range(RH):
                                h = g * RH + r
                                i = mm(bank[2 + s % 2][32 * r:32 * r + 32, g * DH:(g + 1) * DH], bh[:, s % 4, h, :],
                                       up[:, s % 4, h * DH:(h + 1) * DH], start=True, stop=True)
                        i.then_inc(dh_ready, 1)

                    skewed(pe, 4, [(0, turn_u(1)), (-2, add_state)])
                    ph.end()
                    ph.end()

                    def log_decay(c, s):
                        pe.wait_ge(r_ready, n0 + (c + 1))
                        reuse(pe, e_ready, n0, c, 2)
                        for k in range(2):
                            i = mm(bank[2 + s % 2][:, 0:R * Q], after16[:, :], r16[:, s % 2, k, :], start=(k == 0), stop=(k == 1))
                        i.then_inc(d_ready, 1)

                    def turn_c(c, s):
                        pe.wait_ge(ct_ready, n0 + (c + 1))
                        reuse(pe, ch_ready, n0, c, 2)
                        for g in range(HALF):
                            i = mm(bank[4 + s % 2][0:C, g * Q:(g + 1) * Q],
                                   ct[:, s % 2, RH * g:RH * g + RH, :].rearrange("p r n -> p (r n)"), K["fold"],
                                   start=True, stop=True)
                        i.then_inc(c_ready, 1)

                    def outputs(c, s):
                        pe.wait_ge(hbd_ready, n0 + (c + 1))
                        pe.wait_ge(ch_ready, n0 + (c + 1))
                        pe.wait_ge(m_ready, n0 + (c + 1))
                        reuse(pe, y_added, n0, c, 2)
                        b = bank[6 + s % 2]
                        for g in range(HALF):
                            mm(b[0:C, g * Q:(g + 1) * Q], hbd[0:C, s % 4, g, :], ch[0:C, s % 4, g, :], start=True, stop=True)
                            for r in range(RH):
                                h = g * RH + r
                                i = mm(b[32 * r:32 * r + 32, g * Q:(g + 1) * Q], up[:, s % 4, h * DH:(h + 1) * DH],
                                       mk[:, s % 2, :].rearrange("p (t r) -> p r t", r=R)[:, h, :], start=False, stop=True, skip_group_check=True)
                        i.then_inc(yc_ready, 1)

                    skewed(pe, 4, [(0, turn_u(2)), (0, log_decay), (0, turn_c), (-2, outputs)])
                    ph.end()
                for q in range(NG):
                    pe.wait_ge(sq_ready, img * NG + (q + 1))
                    for n in range(GBLK * q, GBLK * (q + 1)):
                        for g in range(HALF):
                            mm(bank[0][:, n:n + 1], y[0:C, g * L + 128 * n:g * L + 128 * n + 128],
                               K["col192"][0:C, :], start=(g == 0), stop=(g == 1))
                        for g in range(HALF):
                            i = mm(bank[0][:, NBLK + n:NBLK + n + 1], ysq[0:C, g * L + 128 * n:g * L + 128 * n + 128],
                                   K["col192"][0:C, :], start=(g == 0), stop=(g == 1))
                i.then_inc(stat_ready, 1)
                for q in range(NG):
                    if q >= 3:
                        pe.wait_ge(fin_done, img * NBLK + GBLK * (q - 2))
                        pe.wait_ge(fin_x, img * NG + (q - 2))
                    b, bx = bank[1 + q % 3], bank[4 + q % 3]
                    for k in range(GBLK):
                        t0 = 128 * (GBLK * q + k)
                        for g in range(HALF):
                            mm(b[:, k * C:(k + 1) * C], y[0:C, g * L + t0:g * L + t0 + 128],
                               woutc[0:C, g, :], start=(g == 0), stop=(g == 1))
                    for k in range(GBLK):
                        t0 = 128 * (GBLK * q + k)
                        if k == 0 and q >= 3:
                            apart(pe)
                        i = nc.tensor.transpose(bx[:, k * C:(k + 1) * C], xT[0:C, t0:t0 + 128], ident(C))
                    i.then_inc(fin_ready, 1)
                ph.end()
                assert ph.k == PHASES, ph.k

        @block.scalar
        def _(act):
            ac = nc.scalar.activation
            ph = Phase(act)
            own = Own(act, act_own, 2, 0)
            act.wait_ge(loads, 16 * NLOAD)
            ac(aneg, aneg, ACT.Exp).then_inc(anegexp, 1)
            ph.end()
            with act.Fori(0, images) as img:
                ph.image(img)
                own.image(img)
                for j in range(8):
                    act.wait_ge(tr_ready, img * 8 + (j + 1))
                    ac(xT3[:, :, 8 * j:8 * j + 8].rearrange("p h w -> p w h"),
                       bank[j % 2][0:C, :].rearrange("p (w h) -> p w h", w=8), ACT.Copy).then_inc(tr_read, 1)

                def evacuate(n, dst, src):
                    act.wait_ge(job_ready, img * JOBS + (n + 1))
                    ac(dst, src, ACT.Copy).then_inc(job_act, 1)

                def norm(k):
                    act.wait_ge(var_ready, img * 2 + (k + 1))
                    own(ac(gvar[0:C, :], gvar[0:C, :], ACT.Ln))
                    ac(rstd[0:C, :], gvar[0:C, :], ACT.Exp, scale=-0.5).then_inc(rstd_ready, 1)

                up_columns(0, evacuate)
                norm(0)
                up_rows(0, evacuate)
                ph.end()
                for t in range(NTILE):
                    if t >= 2:
                        act.wait_ge(proj_ready, img * NTILE + (t - 1))
                    for k in range(KH):
                        act.wait_ge(hid_ready, img * (NTILE * KH) + (KH * t + k + 1))
                        ac(sq[:, t % 2, k, :], bank[3 * (t % 2) + k][:, 0:NROW * GRID], ACT.Square,
                           bias=bias1[:, k:k + 1]).then_inc(hid_sq, 1)
                ph.end()
                down_rows(0, evacuate)
                norm(1)
                ph.end()
                act.wait_ge(pads_ready, img + 1)
                def tanh(g, q):
                    act.wait_ge(conv_done, img * 8 + (4 * g + q + 1))
                    part = slice(g * L + q * QUART, g * L + (q + 1) * QUART)
                    ac(etmp[0:C, part], u[0:C, part], ACT.Tanh).then_inc(tanh_done, 1)

                for g in range(HALF):
                    for k in range(9):
                        if k < 8:
                            act.wait_ge(in_ready, img * 16 + (8 * g + k + 1))
                            ac(xp4[:, g, 1 + 8 * k:9 + 8 * k, 1:1 + W], bank[k % 4][0:C, :].rearrange("p (h w) -> p h w", h=8),
                               ACT.Identity, bias=biasin[0:C, g:g + 1]).then_inc(in_read, 1)
                        if k:
                            j = 8 * g + k - 1
                            act.wait_ge(taps_ready, img * 16 + (j + 1))
                            ac(u4[:, g, 8 * (k - 1):8 * k, :], bank[4 + j % 4][0:C, :].rearrange("p (h w) -> p h w", h=8),
                               ACT.Identity, bias=bconv[0:C, g:g + 1]).then_inc(taps_read, 1)
                        if g == 1 and k >= 5:
                            tanh(0, k - 5)
                for q in range(4):
                    tanh(1, q)
                ph.end()
                for o in range(2):
                    n0 = img * (2 * NC) + o * NC
                    v0 = img * (4 * NC) + o * 2 * NC

                    def copy_u(c, s):
                        reuse(act, tok_ready, n0, c, 4)
                        ac(uc[0:C, s % 4], chunk(u4, o, c), ACT.Copy).then_inc(uc_ready, 1)

                    def copy_u_twice(first):
                        def op(c, s):
                            reuse(act, ut_ready, first, c, 2)
                            ac(ud[0:C, s % 2], chunk(u4, o, c).unsqueeze(2).broadcast_to((C, HALF, 2, Q)),
                               ACT.Copy).then_inc(uc_ready, 1)
                        return op

                    def token_out(c, s):
                        act.wait_ge(tok_ready, n0 + (c + 1))
                        reuse(act, bct_ready, n0, c, 4)
                        reuse(act, tok_kept, n0, c, 4)
                        ac(tk[:, s % 4, :], bank[s % 2][:, 0:NT], ACT.Copy).then_inc(tok_out, 1)

                    skewed(act, 4, [(2, copy_u), (0, token_out)])
                    ph.end()
                    act.wait_ge(abs_ready, img * 2 + (o + 1))
                    ac(expn[:, :], expn[:, :], ACT.Exp, scale=-1.0).then_inc(spe_ready, 1)
                    act.wait_ge(onep_ready, img * 2 + (o + 1))
                    ac(dt[:, :], onep[:, :], ACT.Ln).then_inc(ln_ready, 1)
                    act.wait_ge(cum_ready, img * 2 + (o + 1))
                    ac(tot[0:C, :], bank[2][0:C, 0:NC * R], ACT.Exp)
                    ac(wsuf[:, :], bank[0][:, 0:NC * R], ACT.Exp)
                    ac(ecum[:, :], bank[1][:, 0:NC * R], ACT.Exp).then_inc(cum_exp, 1)
                    ph.end()

                    def state_in(c, s):
                        act.wait_ge(dh_ready, n0 + (c + 1))
                        ac(states(hb)[:, :, one(c + 1)], bank[2 + s % 2][0:C, 0:HALF * DH].unsqueeze(2),
                           ACT.Copy).then_inc(dh_read, 1)

                    skewed(act, 4, [(1, copy_u_twice(v0)), (-2, state_in)])
                    ph.end()
                    if o == 0:
                        for g in range(HALF):
                            ac(y[0:C, g * L:(g + 1) * L], u[0:C, g * L:(g + 1) * L], ACT.Copy, scale=dsum[0:C, g:g + 1])
                    else:
                        ac(xT[0:C, :], xT[0:C, :], ACT.Identity, bias=bcol[0:C, 0:1])
                    ph.end()

                    def decay(c, s):
                        act.wait_ge(d_ready, n0 + (c + 1))
                        reuse(act, m_ready, n0, c, 2)
                        ac(ee[:, s % 2, :], bank[2 + s % 2][:, 0:R * Q], ACT.Exp).then_inc(e_ready, 1)

                    def c_in(c, s):
                        act.wait_ge(c_ready, n0 + (c + 1))
                        reuse(act, yc_ready, n0, c, 4)
                        ac(ch[0:C, s % 4], bank[4 + s % 2][0:C, 0:HALF * Q].rearrange("p (g t) -> p g t", g=HALF),
                           ACT.Copy).then_inc(ch_ready, 1)

                    skewed(act, 4, [(1, copy_u_twice(v0 + NC)), (0, decay), (0, c_in)])
                    ph.end()
                act.sem_inc(u_free, 1)
                part = L // NG
                for q in range(NG):
                    ac(ysq[0:C, :].rearrange("p (g t) -> p g t", g=HALF)[:, :, part * q:part * (q + 1)],
                       y[0:C, :].rearrange("p (g t) -> p g t", g=HALF)[:, :, part * q:part * (q + 1)],
                       ACT.Square).then_inc(sq_ready, 1)
                act.wait_ge(fin_var, img + 1)
                ac(rstds[:, 2, :], rstds[:, 1, :], ACT.Ln).then_inc(fin_ln, 1)
                act.wait_ge(fin_ln, img + 1)
                ac(rstds[:, 3, :], rstds[:, 2, :], ACT.Exp, scale=-0.5).then_inc(fin_rstd, 1)
                for q in range(NG):
                    act.wait_ge(fin_ready, img * NG + (q + 1))
                    if q >= 3:
                        act.wait_ge(fin_done, img * NBLK + GBLK * (q - 2))
                    ac(xsb[:, q % 3, :], bank[4 + q % 3][:, 0:GBLK * C], ACT.Copy).then_inc(fin_x, 1)
                ph.end()
                assert ph.k == PHASES and own.n == 2

        @block.gpsimd
        def _(pool):
            tt = nc.gpsimd.tensor_tensor
            ph = Phase(pool)
            ph.end()
            with pool.Fori(0, images) as img:
                ph.image(img)
                for _ in range(3):
                    ph.end()
                apart(pool)
                for g in range(HALF):
                    nc.gpsimd.memset(xp4[:, g, 0:PW:PW - 1, :], 0.0)
                    i = nc.gpsimd.memset(xp4[:, g, 1:PW - 1, 0:PW:PW - 1], 0.0)
                i.then_inc(pads_ready, 1)
                ph.end()
                for o in range(2):
                    n0 = img * (2 * NC) + o * NC

                    def keep(c, s):
                        pool.wait_ge(tok_out, n0 + (c + 1))
                        apart(pool)
                        nc.gpsimd.tensor_copy(tok3[:, one(c), :], tk[:, s % 4, :].unsqueeze(1)).then_inc(tok_kept, 1)

                    skewed(pool, 4, [(0, keep)])
                    ph.end()
                    ph.end()

                    def weigh(dst, ring, weight, col):
                        def op(c, s):
                            return tt(dst[:, s % ring], rc(weight)[:, one(c), :].rearrange("p c r -> p (c r)").unsqueeze(2)
                                      .broadcast_to((128, R, 2 * N)),
                                      tok3[:, one(c), col:col + 2 * N].broadcast_to((128, R, 2 * N)), ALU.mult)
                        return op

                    def weigh_b(c, s):
                        reuse(pool, dh_ready, n0, c, 4)
                        weigh(bh, 4, wsuf, R)(c, s).then_inc(bh_ready, 1)

                    skewed(pool, 4, [(0, weigh_b)])
                    ph.end()
                    ph.end()

                    def weigh_c(c, s):
                        reuse(pool, c_ready, n0, c, 2)
                        weigh(ct, 2, ecum, R + 2 * N)(c, s).then_inc(ct_ready, 1)

                    def state_out(c, s):
                        reuse(pool, yc_ready, n0, c, 4)
                        tt(hbd[0:C, s % 4].rearrange("p g (r d) -> p r g d", r=RH),
                           states(hf)[:, :, one(c)].rearrange("p (g d) c -> p c g d", g=HALF).broadcast_to((C, RH, HALF, DH)),
                           K["headsel"][0:C, :].unsqueeze(2).unsqueeze(3).broadcast_to((C, RH, HALF, DH)),
                           ALU.mult).then_inc(hbd_ready, 1)

                    skewed(pool, 4, [(0, weigh_c), (0, state_out)])
                    ph.end()
                ph.end()
                assert ph.k == PHASES

        @block.vector
        def _(dve):
            v = nc.vector
            ph = Phase(dve)
            PRO, PER = 7, 89
            own = Own(dve, dve_own, PER, PRO)
            dve.wait_ge(loads, 16 * NLOAD)
            for k in range(KH):
                v.tensor_scalar(w2s[:, k, :], w2t[:, k, :], coef[:, k, 2:3], None, ALU.mult)
                v.tensor_scalar(w2l[:, k, :], w2t[:, k, :], coef[:, k, 1:2], None, ALU.mult)
                v.scalar_tensor_tensor(vconst[:, k:k + 1], b1[:, k:k + 1], coef[:, k, 1:2], coef[:, k, 0:1], ALU.mult, ALU.add)
            for g in range(HALF):
                v.tensor_scalar(woutc[0:C, g, :], wout[0:C, g, :], lng[0:C, g:g + 1], None, ALU.mult)
            v.tensor_reduce(dsum[0:C, :], dsk[0:C], mybir.AxisListType.X, ALU.add).then_inc(w2_scaled, 1)
            v.tensor_scalar(bconv[0:C, :], bconv[0:C, :], 0.5, None, ALU.mult)
            own(v.tensor_scalar(wconv[0:C], wconv[0:C], 0.5, None, ALU.mult))
            for g in range(HALF):
                for t in range(PETAPS[g]):
                    v.tensor_scalar(diag[0:C, g * PETAPS[0] + t, :], K["ident"][0:C, 0:C], wconv[0:C, g, t:t + 1], None, ALU.mult)
            v.tensor_copy(after16[:, :], K["after"])
            v.tensor_copy(tri16[:, :].rearrange("p (t r) -> p t r", r=R), K["tri"].unsqueeze(2).broadcast_to((128, Q, R)))
            dve.wait_ge(anegexp, 1)
            own(v.tensor_scalar(aneg, aneg, -1.0, None, ALU.mult))
            dve.wait_ge(folded, 1)
            own(v.tensor_copy(lin[0:C, :], bank[0][0:C, 0:C]))
            own(v.tensor_tensor(out0[0:C, :], bank[1][0:C, 0:1], b2[0:C, :], ALU.add))
            for g in range(HALF):
                own(v.tensor_tensor(woutc[0:C, g, :], woutc[0:C, g, :], bank[2][0:C, 0:C], ALU.subtract))
            own(v.tensor_copy(bcol[0:C, :], bank[3][0:C, 0:1]))
            ph.end()
            with dve.Fori(0, images) as img:
                ph.image(img)
                own.image(img)

                def evacuate(n, dst, src):
                    dve.wait_ge(job_ready, img * JOBS + (n + 1))
                    v.tensor_copy(dst, src).then_inc(job_dve, 1)

                def norm(k):
                    for j in range(8):
                        i = v.bn_stats(bn[0:C, j, :], xT[0:C, 512 * j:512 * j + 512])
                    own(i)
                    apart(dve)
                    own(v.bn_aggr(mv[0:C, :], bn[0:C]))
                    v.tensor_copy(mom[0:C, 0:1], mv[0:C, 0:1])
                    v.scalar_tensor_tensor(mom[0:C, 1:2], mv[0:C, 0:1], mv[0:C, 0:1], mv[0:C, 1:2],
                                           ALU.mult, ALU.add).then_inc(mom_ready, 1)
                    dve.wait_ge(grp_ready, img * 2 + (k + 1))
                    own(v.tensor_copy(gst[0:C, :], bank[0][0:C, 0:2]))
                    own(v.tensor_tensor(gsq[0:C, :], gst[0:C, 0:1], gst[0:C, 0:1], ALU.mult))
                    own(v.tensor_tensor(gvar[0:C, :], gst[0:C, 1:2], gsq[0:C, :], ALU.subtract))
                    v.tensor_scalar(gvar[0:C, :], gvar[0:C, :], 0.0, 1e-5, ALU.max, ALU.add).then_inc(var_ready, 1)
                    dve.wait_ge(rstd_ready, img * 2 + (k + 1))
                    v.scalar_tensor_tensor(nmr[0:C, :], gst[0:C, 0:1], -1.0, rstd[0:C, :],
                                           ALU.mult, ALU.mult).then_inc(nmr_ready, 1)

                up_columns(1, evacuate)
                dve.wait_ge(tr_read, img * 8 + 8)
                norm(0)
                v.tensor_scalar(w1s[0:C, :], w1t[0:C, :], rstd[0:C, 0:1], None, ALU.mult)
                v.tensor_scalar(lins[0:C, :], lin[0:C, :], rstd[0:C, 0:1], None, ALU.mult)
                dve.wait_ge(shift_ready, img * 2 + 1)
                v.tensor_tensor(bias1[:, :], bank[1][:, 0:KH], b1[:, :], ALU.add)
                v.tensor_tensor(out0i[0:C, :], bank[1][0:C, KH:KH + 1], out0[0:C, :], ALU.add)
                up_rows(1, evacuate)
                ph.end()
                for t in range(NTILE):
                    dve.wait_ge(proj_ready, img * NTILE + (t + 1))
                    v.tensor_copy(z3[:, NROW * t:NROW * (t + 1), :],
                                  bank[6 + t % 2][0:GRID, 0:NROW * C].rearrange("p (h c) -> p h c", h=NROW)).then_inc(proj_read, 1)
                ph.end()
                down_rows(1, evacuate)
                down_columns(img, dve, v)
                dve.wait_ge(job_add, img * 8 + 8)
                norm(1)
                own(v.tensor_scalar(wins[0:C, :], win[0:C, :], rstd[0:C, 0:1], None, ALU.mult))
                dve.wait_ge(shift_ready, img * 2 + 2)
                own(v.tensor_copy(biasin[0:C, :], bank[1][0:C, 0:HALF]))
                ph.end()
                def taps(g, q):
                    dve.wait_ge(taps_read, img * 16 + (8 * g + 2 * q + 2))
                    for t in range(PETAPS[g], 9):
                        src = xp4[:, g, 16 * q + t // 3:16 * (q + 1) + t // 3, t % 3:t % 3 + W]
                        dst = u4[:, g, 16 * q:16 * (q + 1), :]
                        i = v.scalar_tensor_tensor(dst, src, wconv[0:C, g, t:t + 1], dst, ALU.mult, ALU.add)
                        if t < 8:
                            own(i)
                        else:
                            i.then_inc(conv_done, 1)

                def silu(g, q):
                    dve.wait_ge(tanh_done, img * 8 + (4 * g + q + 1))
                    part = slice(g * L + q * QUART, g * L + (q + 1) * QUART)
                    v.scalar_tensor_tensor(u[0:C, part], etmp[0:C, part], 1.0, u[0:C, part], ALU.add, ALU.mult)

                for q in range(4):
                    dve.wait_ge(in_read, img * 16 + min(2 * q + 3, 8))
                    taps(0, q)
                for q in range(4):
                    dve.wait_ge(in_read, img * 16 + (8 + min(2 * q + 3, 8)))
                    taps(1, q)
                    silu(0, q)
                for q in range(4):
                    silu(1, q)
                ph.end()
                dve.wait_ge(stored, img * 16 + 16)
                for o in range(2):
                    n0 = img * (2 * NC) + o * NC
                    v0 = img * (4 * NC) + o * 2 * NC

                    def copy_bc(c, s):
                        dve.wait_ge(bct_ready, n0 + (c + 1))
                        reuse(dve, g_ready, n0, c, 4)
                        v.tensor_copy(bct[0:2 * N, s % 4, :], bank[2 + s % 2][0:2 * N, 0:3 * Q]).then_inc(bct_in, 1)

                    def mask_g(c, s):
                        dve.wait_ge(g_ready, n0 + (c + 1))
                        v.tensor_tensor(gm3[:, one(c), :], bank[4 + s % 2][:, 0:Q].unsqueeze(1), K["tri"].unsqueeze(1),
                                        ALU.mult).then_inc(g_read, 1)

                    skewed(dve, 4, [(-2, copy_bc), (-4, mask_g)])
                    ph.end()
                    own(v.tensor_tensor(rc(dtraw), tok3[:, :, 0:R], dtb[:, o, :].unsqueeze(1).broadcast_to((128, NC, R)), ALU.add))
                    v.scalar_tensor_tensor(expn[:, :], dtraw[:, :], -1.0, dtraw[:, :], ALU.mult, ALU.max).then_inc(abs_ready, 1)
                    dve.wait_ge(spe_ready, img * 2 + (o + 1))
                    v.tensor_scalar(onep[:, :], expn[:, :], 1.0, None, ALU.add).then_inc(onep_ready, 1)
                    dve.wait_ge(onep_ready, img * 2 + (o + 1))
                    own(v.tensor_scalar(den[:, :], onep[:, :], -1.0, None, ALU.add))
                    own(v.tensor_scalar(tiny[:, :], den[:, :], 0.0, None, ALU.is_equal))
                    own(v.tensor_tensor(den[:, :], den[:, :], tiny[:, :], ALU.add))
                    own(v.reciprocal(den[:, :], den[:, :]))
                    own(v.tensor_tensor(den[:, :], den[:, :], expn[:, :], ALU.mult))
                    own(v.tensor_tensor(tiny[:, :], tiny[:, :], expn[:, :], ALU.mult))
                    dve.wait_ge(ln_ready, img * 2 + (o + 1))
                    own(v.tensor_tensor(dt[:, :], dt[:, :], den[:, :], ALU.mult))
                    own(v.tensor_tensor(dt[:, :], dt[:, :], tiny[:, :], ALU.add))
                    own(v.scalar_tensor_tensor(dt[:, :], dtraw[:, :], 0.0, dt[:, :], ALU.max, ALU.add))
                    v.tensor_tensor(rc(aa), rc(dt), aneg[:, o, :].unsqueeze(1).broadcast_to((128, NC, R)),
                                    ALU.mult).then_inc(aa_ready, 1)
                    dve.wait_ge(aa_ready, img * 2 + (o + 1))
                    own(v.tensor_scalar(aclip[:, :], aa[:, :], -1000.0, None, ALU.max))
                    own(v.tensor_copy(ahi[:, :], aclip[:, :]))
                    v.tensor_tensor(alo[:, :], aclip[:, :], ahi[:, :], ALU.subtract)
                    dve.wait_ge(cum_exp, img * 2 + (o + 1))
                    own(v.tensor_tensor(tot[0:C, :].rearrange("p (n r) -> p n r", r=RH), tot[0:C, :].rearrange("p (n r) -> p n r", r=RH),
                                        K["headsel"][0:C, :].unsqueeze(1).broadcast_to((C, HALF * NC, RH)), ALU.mult))
                    own(v.tensor_reduce(dec[0:C, :], tot[0:C, :].rearrange("p (n r) -> p n r", r=RH), mybir.AxisListType.X, ALU.add))
                    ph.end()

                    def scale_u(phase):
                        def op(c, s):
                            dve.wait_ge(ut_ready, v0 + (phase * NC + c + 1))
                            reuse(dve, dh_ready if phase == 0 else yc_ready, n0, c, 4)
                            v.tensor_tensor(up[:, s % 4].rearrange("p (r d) -> p r d", r=R),
                                            bank[s % 2][:, 0:R * DH].rearrange("p (r d) -> p r d", r=R),
                                            rc(dt)[:, one(c), :].rearrange("p c r -> p (c r)").unsqueeze(2).broadcast_to((128, R, DH)),
                                            ALU.mult).then_inc(up_ready, 1)
                        return op

                    skewed(dve, 4, [(0, scale_u(0))])
                    own(v.memset(decx[0:C, :], 0.0))
                    v.memset(states(hb)[:, :, 0:1], 0.0)
                    v.memset(hb[0:C, NST - 1:NST], 0.0)
                    dec3 = dec[0:C, :].rearrange("p (c g) -> p g c", g=HALF)
                    for g in range(HALF):
                        v.tensor_copy(states(decx)[:, g * DH:(g + 1) * DH, 1:SLOT],
                                      dec3[:, g:g + 1, :].broadcast_to((C, DH, NC)))
                    ph.end()
                    own(v.tensor_tensor_scan(hf[0:C, :], decx[0:C, :], hb[0:C, :], 0.0, ALU.mult, ALU.add))
                    own(v.tensor_tensor_scan(hb[0:C, ::-1], decx[0:C, ::-1], hb[0:C, ::-1], 0.0, ALU.mult, ALU.add))
                    own(v.tensor_scalar(hf[0:C, 0:NST - 2], hf[0:C, 0:NST - 2], K["fwd"][0:C, :], None, ALU.mult))
                    own(v.scalar_tensor_tensor(hf[0:C, 0:NST - 2], hb[0:C, 2:NST], K["bwd"][0:C, :], hf[0:C, 0:NST - 2],
                                               ALU.mult, ALU.add))
                    ph.end()

                    def spread_a(c, s):
                        reuse(dve, d_ready, n0, c, 2)
                        for k, part in enumerate((ahi, alo)):
                            i = v.tensor_tensor(r16[:, s % 2, k].rearrange("p (t r) -> p t r", r=R),
                                                rc(part)[:, one(c), :].broadcast_to((128, Q, R)),
                                                tri16[:, :].rearrange("p (t r) -> p t r", r=R), ALU.mult)
                        i.then_inc(r_ready, 1)

                    def weigh_g(c, s):
                        dve.wait_ge(e_ready, n0 + (c + 1))
                        reuse(dve, yc_ready, n0, c, 2)
                        v.tensor_tensor(mk[:, s % 2].rearrange("p (t r) -> p t r", r=R), ee[:, s % 2].rearrange("p (t r) -> p t r", r=R),
                                        gm3[:, one(c), :].rearrange("p c t -> p (c t)").unsqueeze(2).broadcast_to((128, Q, R)),
                                        ALU.mult).then_inc(m_ready, 1)

                    def add_y(c, s):
                        dve.wait_ge(yc_ready, n0 + (c + 1))
                        yy = chunk(y4, o, c)
                        v.tensor_tensor(yy, yy, bank[6 + s % 2][0:C, 0:HALF * Q].rearrange("p (g t) -> p g t", g=HALF),
                                        ALU.add).then_inc(y_added, 1)

                    skewed(dve, 4, [(1, spread_a), (0, scale_u(1)), (-1, weigh_g), (-3, add_y)])
                    ph.end()

                dve.wait_ge(stat_ready, img + 1)
                own(v.tensor_copy(rstds[:, 0, :], bank[0][:, 0:NBLK]))
                own(v.tensor_tensor(rstds[:, 0, :], rstds[:, 0, :], rstds[:, 0, :], ALU.mult))
                own(v.tensor_tensor(rstds[:, 1, :], bank[0][:, NBLK:2 * NBLK], rstds[:, 0, :], ALU.subtract))
                v.tensor_scalar(rstds[:, 1, :], rstds[:, 1, :], 0.0, 1e-5, ALU.max, ALU.add).then_inc(fin_var, 1)
                dve.wait_ge(fin_rstd, img + 1)
                for n in range(NBLK):
                    q, k = divmod(n, GBLK)
                    if k == 0:
                        dve.wait_ge(fin_x, img * NG + (q + 1))
                    v.scalar_tensor_tensor(ot[:, n * C:(n + 1) * C], bank[1 + q % 3][:, k * C:(k + 1) * C],
                                           rstds[:, 3, n:n + 1], xsb[:, q % 3, k * C:(k + 1) * C],
                                           ALU.mult, ALU.add).then_inc(fin_done, 1)
                ph.end()
                assert ph.k == PHASES and own.n == PRO + PER, own.n

    return nc


def constants():
    import numpy as np

    theta = 2 * np.pi * (np.arange(GRID) + 0.25) / GRID
    pos = 2 * np.pi * np.arange(W) / W
    freq = np.arange(-W // 2, W // 2 + 1)
    phase = np.exp(1j * freq[:, None, None] * (theta[None, :, None] - pos[None, None, :]))
    edge = np.where(abs(freq) == W // 2, 0.5, 1.0)[:, None, None]
    col = {
        "up": (phase.sum(0).real / W).T,
        "down": (phase * edge).sum(0).real / GRID,
        "ident": np.eye(128),
        "fold": np.tile(np.eye(Q), (2, 1)),
    }
    j = np.arange(Q)
    two = np.zeros((2, Q, 2, Q))
    two[0, :, 0] = j[:, None] > j[None, :]
    two[1, :, 1] = j[:, None] < j[None, :]
    col["after"] = two.reshape(128, 128)
    two = np.zeros((2, Q, 2, Q))
    two[0, :, 0] = j[:, None] <= j[None, :]
    two[1, :, 1] = j[:, None] >= j[None, :]
    col["upto"] = two.reshape(128, 128)
    col["tri"] = np.concatenate([two[0, :, 0], two[1, :, 1]])
    p = np.arange(C)
    direction = p % (2 * N) // N
    col["dirsum"] = np.repeat(np.arange(2), Q)[:, None] == direction[None, :]
    col["group"] = (p[:, None] // GROUP == p[None, :] // GROUP) / GROUP
    col["headsel"] = p[:, None] // (2 * N) == np.arange(RH)[None, :]
    col["fwd"] = (direction == 0)[:, None]
    col["bwd"] = (direction == 1)[:, None]
    col["mean192"] = np.full((C, C), 1.0 / DI)
    col["col192"] = np.full((C, 1), 1.0 / DI)
    out = np.zeros((128, CONST_N), np.float32)
    for name, v in col.items():
        s, e = CONST_AT[name]
        assert v.shape[1] == e - s, name
        out[:v.shape[0], s:e] = v
    return out


def laid_out(inputs):
    import numpy as np

    i = {k: np.asarray(v) for k, v in inputs.items()}
    xp = i["L1_conv_x_proj_weight"]
    wtok = np.zeros((2, 2, DI, NT), np.float32)
    for o in range(2):
        for d in range(2):
            w = xp[o + 2 * d].T
            wtok[o, d, :, 0:R] = w[:, 0:R]
            wtok[o, d, :, R + d * N:R + (d + 1) * N] = w[:, R:R + N]
            wtok[o, d, :, R + (2 + d) * N:R + (3 + d) * N] = w[:, R + N:R + 2 * N]

    def cols(v, p):
        return v.reshape(-1, p).T

    arrays = {
        "x": i["x"], "consts": constants(), "W1": i["L0_conv_W1"], "W1T": i["L0_conv_W1"].T, "W2T": i["L0_conv_W2"].T,
        "b1": cols(i["L0_conv_b1"], 128), "b2": cols(i["L0_conv_b2"], C), "coef": i["L0_conv_coef"], "w_in": i["L1_conv_w_in"],
        "w_conv": i["L1_conv_w_conv"].reshape(9, DI).T, "b_conv": cols(i["L1_conv_b_conv"], C), "wtok": wtok,
        "A_logs": i["L1_conv_A_logs"], "dt_bias": i["L1_conv_dt_bias"], "Ds": i["L1_conv_Ds"].reshape(4, DI).T,
        "ln_g": cols(i["L1_conv_ln_g"], C), "ln_b": cols(i["L1_conv_ln_b"], C), "w_out": i["L1_conv_w_out"],
    }
    return {f"in_{k}": np.ascontiguousarray(v) for k, v in arrays.items()}


def kernel(**inputs):
    import concourse.bacc as bacc
    from concourse.bass_utils import run_bass_kernel_spmd

    nc = bacc.Bacc("TRN2", target_bir_lowering=False, num_devices=1)
    arrays = laid_out(inputs)
    aps = {k[3:]: nc.dram_tensor(k, v.shape, mybir.dt.from_np(v.dtype), kind="ExternalInput").ap() for k, v in arrays.items()}
    out = nc.dram_tensor("out", (B, H, W, C), F32, kind="ExternalOutput").ap()
    build(nc, aps, out)
    r = run_bass_kernel_spmd(nc, [arrays], core_ids=[0])
    return r.results[0]["out"]
```

```python
from contextlib import ExitStack

import concourse.bass as bass
from concourse import mybir

F32 = mybir.dt.float32
F16 = mybir.dt.float16
ALU = mybir.AluOpType
ACT = mybir.ActivationFunctionType

B, H, W, C = 16, 64, 64, 96
L = H * W
GROUP = 3
HID = 4 * C
KH = HID // 128
GRID = 96
DI = 192
HALF = 2
R, DH, N = 6, 32, 16
RH = R // HALF
Q = 64
NC = L // Q
ND = R + 2 * N
NT = R + 4 * N
SLOT = NC + 1
NST = HALF * DH * SLOT + 1
NROW = 4
NTILE = GRID // NROW
PERBANK = 5
NJOB = -(-C // PERBANK)
NBLK = L // 128
GBLK = 4
NG = NBLK // GBLK
BBLK = 5
NBANK = 6
CB = 8
TB = 8
LAG = 2
WARM1, WARM2 = 2, 5
KEEP = 256
PETAPS = (3, 3)
QUART = L // 4

CONST_PARTS = [("up", GRID), ("down", W), ("ident", 128), ("fold", Q), ("after", 128), ("upto", 128),
               ("dirsum", C), ("tri", Q), ("group", C), ("headsel", RH), ("fwd", 1), ("bwd", 1),
               ("mean192", C), ("col192", 1)]
CONST_AT, CONST_N = {}, 0
for _name, _n in CONST_PARTS:
    CONST_AT[_name] = (CONST_N, CONST_N + _n)
    CONST_N += _n


def build(nc, a, out, images=B):
    ctx = ExitStack()
    with ctx:
        def sb(name, n, dt=F32):
            return ctx.enter_context(nc.sbuf_tensor(name, [128, n], dt))

        def sem(name):
            return ctx.enter_context(nc.semaphore(name))

        bank = [ctx.enter_context(nc.psum_tensor(f"bank{i}", [128, 512], F32)) for i in range(8)]

        cst = sb("cst", CONST_N)
        K = {k: cst[:, s:e] for k, (s, e) in CONST_AT.items()}
        assert CONST_N >= 512
        w1t = sb("w1t", HID)
        w1s = sb("w1s", HID)
        w2s = sb("w2s", KH * C)[:, :].rearrange("p (k c) -> p k c", k=KH)
        lin = sb("lin", C)
        lins = sb("lins", C)
        coef = sb("coef", KH * 3)[:, :].rearrange("p (k c) -> p k c", k=KH)
        b1 = sb("b1", KH)
        vconst = sb("vconst", KH)
        b2 = sb("b2", 1)
        out0 = sb("out0", 1)
        win = sb("win", DI)
        wins = sb("wins", DI)
        wconv = sb("wconv", HALF * 9)[:, :].rearrange("p (g t) -> p g t", g=HALF)
        bconv = sb("bconv", HALF)
        diag = sb("diag", sum(PETAPS) * C)[:, :].rearrange("p (k c) -> p k c", c=C)
        wtok = sb("wtok", 2 * HALF * 2 * ND)[:, :].rearrange("p (o g n) -> p o g n", o=2, g=HALF)
        wbc = sb("wbc", 2 * HALF * 128)[:, :].rearrange("p (o g n) -> p o g n", o=2, g=HALF)
        dtb = sb("dtb", 2 * R)[:, :].rearrange("p (o r) -> p o r", o=2)
        aneg = sb("aneg", 2 * R)[:, :].rearrange("p (o r) -> p o r", o=2)
        dsk = sb("dsk", HALF * 4)[:, :].rearrange("p (g k) -> p g k", g=HALF)
        dsum = sb("dsum", HALF)
        lng = sb("lng", HALF)
        lnb = sb("lnb", HALF)
        woutc = sb("woutc", HALF * (C + 1))[:, :].rearrange("p (g c) -> p g c", g=HALF)
        bcol = sb("bcol", 1)
        after16 = sb("after16", 128, F16)
        zero16 = sb("zero16", Q * R, F16)
        tri16 = sb("tri16", Q * R, F16)
        bn = sb("bn", 8 * 6)[:, :].rearrange("p (k s) -> p k s", s=6)
        mv = sb("mv", 2)
        mom = sb("mom", 2)
        gst = sb("gst", 2)
        gsq = sb("gsq", 1)
        gvar = sb("gvar", 1)
        rstd = sb("rstd", 1)
        nmr = sb("nmr", 1)
        bias1 = sb("bias1", KH)
        out0i = sb("out0i", 1)
        biasin = sb("biasin", HALF)
        dt = sb("dt", NC * R)
        aa = sb("aa", NC * R)
        a16 = sb("a16", 2 * NC * R, F16)[:, :].rearrange("p (k n) -> p k n", k=2)
        r16 = sb("r16", 2 * 2 * Q * R, F16)[:, :].rearrange("p (s k n) -> p s k n", s=2, k=2)
        rstds = sb("rstds", 4 * NBLK)[:, :].rearrange("p (i n) -> p i n", i=4)
        wsuf = sb("wsuf", NC * R)
        ecum = sb("ecum", NC * R)
        tot = sb("tot", NC * R)
        dec = sb("dec", HALF * NC)
        xT = sb("xT", L)
        ARENA = 40393
        arena = sb("arena", ARENA)
        QUIET = 2 * HALF * L + HALF * (W + 2) * (W + 2)
        at = [0]

        def take(n, start=None):
            if start is not None:
                at[0] = start
            v = arena[:, at[0]:at[0] + n]
            at[0] += n
            assert at[0] <= ARENA, at
            return v

        w1n = take(KH * C, 30000).rearrange("p (k c) -> p k c", k=KH)
        w2t = take(KH * C).rearrange("p (k c) -> p k c", k=KH)
        w2l = take(KH * C).rearrange("p (k c) -> p k c", k=KH)
        wout = take(HALF * C).rearrange("p (g c) -> p g c", g=HALF)
        xs = take(W * C, 0)
        y1 = xs
        st_a = take(GRID * C)
        z = st_a
        xu = take(GRID * GRID)
        sq = take(2 * KH * NROW * GRID, QUIET).rearrange("p (s k n) -> p s k n", s=2, k=KH)
        PW = W + 2
        u = take(HALF * L, 0)
        y = take(HALF * L)
        etmp = y
        state_at = at[0]
        hf = take(NST)
        hb = take(NST)
        tokp = take(NC * NT, QUIET)
        gm_at = at[0]
        xpad = take(HALF * PW * PW, state_at)
        ysq = take(HALF * L, state_at)
        gm = take(NC * Q, gm_at)
        ring_at0 = at[0]
        bct = take(2 * 4 * CB * Q, state_at).rearrange("p (k g t) -> p k g t", k=2, g=4)
        dtraw, expn, onep, den, tiny, aclip = (take(NC * R, ring_at0 + k * NC * R) for k in range(6))
        ud = take(4 * HALF * 2 * Q, ring_at0).rearrange("p (s g k t) -> p s g k t", s=4, g=HALF, k=2)
        bh_at = at[0]
        bh = take(4 * R * 2 * N).rearrange("p (s r n) -> p s r n", s=4, r=R)
        ct = take(2 * R * 2 * N, bh_at).rearrange("p (s r n) -> p s r n", s=2, r=R)
        take(2 * R * 2 * N)
        up = take(4 * R * DH).rearrange("p (s n) -> p s n", s=4)
        ring_at = at[0]
        ee = take(2 * R * Q).rearrange("p (s n) -> p s n", s=2)
        mk = take(2 * R * Q).rearrange("p (s n) -> p s n", s=2)
        ch = take(4 * HALF * Q).rearrange("p (s g t) -> p s g t", s=4, g=HALF)
        hbd = take(4 * HALF * C).rearrange("p (s g n) -> p s g n", s=4, g=HALF)
        decx = take(NST, ring_at)
        ot = take(NBLK * C, gm_at)

        xs3 = xs[0:H, :].rearrange("p (w c) -> p w c", w=W)
        xs3p = xs.rearrange("p (w c) -> p w c", w=W)
        st_a3p = st_a.rearrange("p (c h) -> p c h", c=C)
        z3p = z.rearrange("p (h c) -> p h c", h=GRID)
        y13p = y1.rearrange("p (c w) -> p c w", c=C)
        sta3 = st_a[0:W, :].rearrange("p (c h) -> p c h", c=C)
        xu3 = xu[0:C, :].rearrange("p (h w) -> p h w", h=GRID)
        z3 = z[0:GRID, :].rearrange("p (h c) -> p h c", h=GRID)
        y13 = y1[0:GRID, :].rearrange("p (c w) -> p c w", c=C)
        xT3 = xT[0:C, :].rearrange("p (h w) -> p h w", h=H)
        u4 = u[0:C, :].rearrange("p (g h w) -> p g h w", g=HALF, h=H)
        y4 = y[0:C, :].rearrange("p (g h w) -> p g h w", g=HALF, h=H)
        xp4 = xpad[0:C, :].rearrange("p (g h w) -> p g h w", g=HALF, h=PW)
        xp4p, u4p = (t.rearrange("p (g h w) -> p g h w", g=HALF, w=n) for t, n in ((xpad, PW), (u, W)))
        tok3 = tokp.rearrange("p (c n) -> p c n", c=NC)
        gm3 = gm.rearrange("p (c t) -> p c t", c=NC)

        def rc(t):
            return t[:, :].rearrange("p (c r) -> p c r", c=NC)

        def states(t, shift=0):
            return t[0:C, shift:shift + HALF * DH * SLOT].rearrange("p (n c) -> p n c", c=SLOT)

        def one(c):
            return slice(c, c + 1) if isinstance(c, int) else bass.ds(c, 1)

        def chunk(t4, o, c):
            v = t4[:, :, one(c), :] if o == 0 else t4[:, :, :, one(c)]
            return v.rearrange("p g a b -> p g (a b)")

        loads, x_in, u_free, stored = sem("loads"), sem("x_in"), sem("u_free"), sem("stored")
        waited = sem("waited")
        phase_done = sem("phase_done")
        dve_own, act_own = sem("dve_own"), sem("act_own")
        st_padded = sem("st_padded")
        w2_scaled, folded, anegexp = sem("w2_scaled"), sem("folded"), sem("anegexp")
        mom_ready, grp_ready, var_ready = sem("mom_ready"), sem("grp_ready"), sem("var_ready")
        rstd_ready, nmr_ready, shift_ready = sem("rstd_ready"), sem("nmr_ready"), sem("shift_ready")
        tr_ready, tr_act, tr_dve = sem("tr_ready"), sem("tr_act"), sem("tr_dve")
        job_ready, job_act, job_dve, job_add = sem("job_ready"), sem("job_act"), sem("job_dve"), sem("job_add")
        hid_ready, hid_sq, proj_ready, proj_read = sem("hid_ready"), sem("hid_sq"), sem("proj_ready"), sem("proj_read")
        in_ready, in_read, pads_ready = sem("in_ready"), sem("in_read"), sem("pads_ready")
        taps_ready, taps_read, conv_done, tanh_done, silu_done = sem("taps_ready"), sem("taps_read"), sem("conv_done"), sem("tanh_done"), sem("silu_done")
        abs_ready, spe_ready, onep_ready, ln_ready = sem("abs_ready"), sem("spe_ready"), sem("onep_ready"), sem("ln_ready")
        aa_ready, cum_ready, cum_exp = sem("aa_ready"), sem("cum_ready"), sem("cum_exp")
        fwd_scanned, fwd_masked = sem("fwd_scanned"), sem("fwd_masked")
        uc_ready = sem("uc_ready")
        tok_ready, tok_out = sem("tok_ready"), sem("tok_out")
        bc_ready, b_moved, c_moved, g_ready, g_read = sem("bc_ready"), sem("b_moved"), sem("c_moved"), sem("g_ready"), sem("g_read")
        ut_ready, up_ready = sem("ut_ready"), sem("up_ready")
        bh_ready, dh_ready, dh_read = sem("bh_ready"), sem("dh_ready"), sem("dh_read")
        r_ready, d_ready, e_ready, m_ready = sem("r_ready"), sem("d_ready"), sem("e_ready"), sem("m_ready")
        ct_ready, c_ready, ch_ready = sem("ct_ready"), sem("c_ready"), sem("ch_ready")
        hbd_ready, yc_ready, y_added = sem("hbd_ready"), sem("yc_ready"), sem("y_added")
        xt_ready, xt_act, xt_dve, sq_done = sem("xt_ready"), sem("xt_act"), sem("xt_dve"), sem("sq_done")
        fin_ready, fin_var, fin_ln, fin_rstd = (sem(n) for n in ("fin_ready", "fin_var", "fin_ln", "fin_rstd"))
        fin_done, sq_ready = sem("fin_done"), sem("sq_ready")

        ENGINES = 4
        PHASES = 14
        JOBS = 2 * NJOB + 12 + 8
        NLOAD = 26

        def apart(eng):
            eng.sem_inc(waited, 1)

        class Phase:

            def __init__(self, eng):
                self.eng, self.k, self.img = eng, 0, None

            def image(self, img):
                self.k, self.img = 0, img

            def end(self):
                self.k += 1
                apart(self.eng)
                self.eng.drain().then_inc(phase_done, 1)
                if self.img is None:
                    self.eng.wait_ge(phase_done, ENGINES * self.k)
                else:
                    self.eng.wait_ge(phase_done, self.img * (ENGINES * PHASES) + ENGINES * (self.k + 1))

        class Own:

            def __init__(self, eng, s, per, pro):
                self.eng, self.s, self.per, self.pro, self.n, self.img = eng, s, per, pro, 0, None

            def image(self, img):
                assert self.n == self.pro, self.n
                self.img = img

            def __call__(self, ins):
                ins.then_inc(self.s, 1)
                self.n += 1
                self.eng.wait_ge(self.s, self.n if self.img is None else self.img * self.per + self.n)

        def skewed(eng, unroll, ops):
            lo, hi = min(s for s, _ in ops), max(s for s, _ in ops)
            start = -(-(4 - lo) // unroll) * unroll
            stop = (NC - hi) // unroll * unroll

            def step(t, k):
                for s, op in ops:
                    if not isinstance(t, int) or 0 <= t + s < NC:
                        op(t + s, k + s)
            for t in range(-hi, start):
                step(t, t)
            with eng.Fori(start, stop - unroll + 1, unroll) as i:
                for j in range(unroll):
                    step(i + j, j)
            for t in range(stop, NC - lo):
                step(t, t)

        def reuse(eng, s, first, c, ring):
            if not isinstance(c, int) or c >= ring:
                eng.wait_ge(s, first + (c - (ring - 1)))

        def ident(n):
            return K["ident"][0:n, 0:n]

        def jobs(first, count, mine, read, after={}):
            for j in range(count):
                if (first + j) % 2 == mine:
                    read(first + j, j, bank[2 + (first + j) % NBANK])
                if j in after:
                    after[j]()

        def up_columns(mine, evacuate, after={}):
            def read(n, j, b):
                k = min(PERBANK, C - j * PERBANK)
                evacuate(n, sta3[:, j * PERBANK:j * PERBANK + k, :], b[0:W, 0:k * GRID].rearrange("p (c h) -> p c h", c=k))
            jobs(0, NJOB, mine, read, after)

        def up_rows(mine, evacuate, after={}):
            def read(n, j, b):
                k = min(PERBANK, GRID - j * PERBANK)
                evacuate(n, xu3[:, j * PERBANK:j * PERBANK + k, :], b[0:C, 0:k * GRID].rearrange("p (h w) -> p h w", h=k))
            jobs(NJOB, NJOB, mine, read, after)

        def down_rows(mine, evacuate):
            def read(n, j, b):
                evacuate(n, y13[:, 8 * j:8 * j + 8, :], b[0:GRID, 0:8 * W].rearrange("p (c w) -> p c w", c=8))
            jobs(2 * NJOB, 12, mine, read)

        def down_columns(img, dve, v, stats):
            for j in range(8):
                n = 2 * NJOB + 12 + j
                dve.wait_ge(job_ready, img * JOBS + (n + 1))
                dst = xT3[:, :, 8 * j:8 * j + 8].rearrange("p h w -> p w h")
                v.scalar_tensor_tensor(dst, bank[2 + n % NBANK][0:C, :].rearrange("p (w h) -> p w h", w=8), out0i[0:C, 0:1], dst,
                                       ALU.add, ALU.add).then_inc(job_add, 1)
                if j:
                    dve.wait_ge(job_add, img * 8 + j)
                    stats(j - 1)
            dve.wait_ge(job_add, img * 8 + 8)
            return stats(7)

        block = ctx.enter_context(nc.Block())

        @block.sync
        def _(sp):
            n = [0]

            def load(dst, src):
                sp.dma_start(dst, src).then_inc(loads, 16)
                n[0] += 1

            load(cst[:, :], a["consts"])
            load(w1n, a["W1"].rearrange("(k p) c -> p k c", p=128))
            load(w1t[0:C, :], a["W1T"])
            load(w2t, a["W2T"].rearrange("(k p) c -> p k c", p=128))
            load(coef, a["coef"].rearrange("(k p) c -> p k c", p=128))
            load(b1[:, :], a["b1"])
            load(b2[0:C, :], a["b2"])
            load(win[0:C, :], a["w_in"])
            load(wconv[0:C], a["w_conv"].rearrange("(g p) t -> p g t", g=HALF))
            load(bconv[0:C, :], a["b_conv"])
            load(dsk[0:C], a["Ds"].rearrange("(g p) k -> p g k", g=HALF))
            load(lng[0:C, :], a["ln_g"])
            load(lnb[0:C, :], a["ln_b"])
            load(wout[0:C], a["w_out"].rearrange("(g p) c -> p g c", g=HALF))
            for o in range(2):
                load(wbc[0:C, o], a["wbc"][o].rearrange("(g p) n -> p g n", g=HALF))
                load(wtok[0:C, o], a["wtok"][o].rearrange("(g p) n -> p g n", g=HALF))
                for d in range(2):
                    k = o + 2 * d
                    load(dtb[Q * d:Q * d + Q, o, :], a["dt_bias"][k:k + 1, :].broadcast_to((Q, R)))
                    load(aneg[Q * d:Q * d + Q, o, :], a["A_logs"][k:k + 1, :].broadcast_to((Q, R)))
            assert n[0] == NLOAD, n
            sp.sem_inc(stored, 16)

            def load_x(n):
                sp.dma_start(xs3, a["x"][n].rearrange("b h w c -> (b h) w c")).then_inc(x_in, 16)

            def store(n):
                sp.dma_start(out[n].rearrange("b h w c -> (b h w) c").rearrange("(n p) c -> p n c", p=128),
                             ot.rearrange("p (n c) -> p n c", c=C)).then_inc(stored, 16)

            load_x(slice(0, 1))
            if images > 1:
                with sp.Fori(0, images - 1) as img:
                    sp.wait_ge(u_free, img + 1)
                    load_x(bass.ds(img + 1, 1))
                    sp.wait_ge(fin_done, img * NBLK + NBLK)
                    store(bass.ds(img, 1))
            sp.wait_ge(fin_done, images * NBLK)
            store(slice(images - 1, images))
            sp.wait_ge(stored, 16 * images + 16)

        @block.tensor
        def _(pe):
            mm = nc.tensor.matmul

            def warm(n):
                for _ in range(n):
                    mm(bank[7][:, :], K["after"], cst[:, 0:512], start=True, stop=True)

            def keep_warm():
                mm(bank[7][:, 0:KEEP], after16[:, :], zero16[:, 0:KEEP], start=True, stop=True)

            ph = Phase(pe)
            pe.wait_ge(loads, 16 * NLOAD)
            pe.wait_ge(w2_scaled, 1)
            for k in range(KH):
                mm(bank[0][0:C, 0:C], w1n[:, k, :], w2l[:, k, :], start=(k == 0), stop=(k == KH - 1))
            for k in range(KH):
                mm(bank[1][0:C, 0:1], w2t[:, k, :], vconst[:, k:k + 1], start=(k == 0), stop=(k == KH - 1))
            for g in range(HALF):
                mm(bank[2][0:C, 0:C], K["mean192"][0:C, :], woutc[0:C, g, 0:C], start=(g == 0), stop=(g == 1))
            for g in range(HALF):
                i = mm(bank[3][0:C, 0:1], wout[0:C, g, :], lnb[0:C, g:g + 1], start=(g == 0), stop=(g == 1))
            i.then_inc(folded, 1)
            ph.end()
            with pe.Fori(0, images) as img:
                ph.image(img)
                pe.wait_ge(x_in, img * 16 + 16)
                for j in range(8):
                    if j >= 4:
                        pe.wait_ge((tr_act, tr_dve)[j % 2], img * 4 + (j // 2 - 1))
                    apart(pe)
                    for k in range(8):
                        i = nc.tensor.transpose(bank[j % 4][0:C, k * H:(k + 1) * H], xs3[:, 8 * j + k, :], ident(H))
                    i.then_inc(tr_ready, 1)
                job = [0]

                def drained(n):
                    if n >= JOBS - 8:
                        pe.wait_ge(job_add, img * 8 + (n - (JOBS - 8) + 1))
                    else:
                        pe.wait_ge(job_act if n % 2 == 0 else job_dve, img * ((JOBS - 8) // 2) + (n // 2 + 1))

                def resample(count, per_bank, product, before={}):
                    for j in range(-(-count // per_bank)):
                        if j in before:
                            before[j]()
                        n = job[0]
                        if n >= NBANK:
                            drained(n - NBANK)
                            apart(pe)
                        for k in range(j * per_bank, min(count, (j + 1) * per_bank)):
                            i = product(bank[2 + n % NBANK], k - j * per_bank, k)
                        i.then_inc(job_ready, 1)
                        job[0] += 1

                def all_drained():
                    for n in range(job[0] - NBANK, job[0]):
                        drained(n)

                def group_means(k):
                    pe.wait_ge(mom_ready, img * 2 + (k + 1))
                    mm(bank[0][0:C, 0:2], K["group"][0:C, :], mom[0:C, :], start=True, stop=True).then_inc(grp_ready, 1)

                def shifts(k, shift):
                    pe.wait_ge(nmr_ready, img * 2 + (k + 1))
                    shift().then_inc(shift_ready, 1)

                def shift_hidden():
                    for k in range(KH):
                        mm(bank[1][:, k:k + 1], w1t[0:C, 128 * k:128 * k + 128], nmr[0:C, :], start=True, stop=True)
                    return mm(bank[1][0:C, KH:KH + 1], lin[0:C, :], nmr[0:C, :], start=True, stop=True)

                def shift_in():
                    for g in range(HALF):
                        i = mm(bank[1][0:C, g:g + 1], win[0:C, C * g:C * g + C], nmr[0:C, :], start=True, stop=True)
                    return i

                pe.wait_ge(tr_act, img * 4 + 4)
                pe.wait_ge(tr_dve, img * 4 + 4)
                apart(pe)
                resample(C, PERBANK, lambda b, k, c: mm(
                    b[0:W, k * GRID:(k + 1) * GRID], xs3p[:, :, c], K["up"], start=True, stop=True))
                all_drained()
                pe.wait_ge(st_padded, img + 1)
                apart(pe)
                resample(GRID, PERBANK, lambda b, k, h: mm(
                    b[0:C, k * GRID:(k + 1) * GRID], st_a3p[:, :, h], K["up"], start=True, stop=True),
                    before={9: lambda: group_means(0), 17: lambda: shifts(0, shift_hidden)})
                all_drained()
                ph.end()

                def hidden(t):
                    if t >= 2:
                        pe.wait_ge(hid_sq, img * (NTILE * KH) + KH * (t - 1))
                    for k in range(KH):
                        mm(bank[3 * (t % 2) + k][:, 0:NROW * GRID], w1s[0:C, 128 * k:128 * k + 128],
                           xu3[:, NROW * t:NROW * (t + 1), :], start=True, stop=True).then_inc(hid_ready, 1)

                def project(t):
                    pe.wait_ge(hid_sq, img * (NTILE * KH) + KH * (t + 1))
                    if t >= 2:
                        pe.wait_ge(proj_read, img * NTILE + (t - 1))
                    for h in range(NROW):
                        o = bank[6 + t % 2][0:GRID, h * C:(h + 1) * C]
                        mm(o, xu3[:, NROW * t + h, :], lins[0:C, :], start=True, stop=False)
                        for k in range(KH):
                            i = mm(o, sq[:, t % 2, k, h * GRID:(h + 1) * GRID], w2s[:, k, :], start=False, stop=(k == KH - 1))
                    i.then_inc(proj_ready, 1)

                for t in range(NTILE):
                    hidden(t)
                    if t:
                        project(t - 1)
                project(NTILE - 1)
                ph.end()
                resample(C, 8, lambda b, k, c: mm(
                    b[0:GRID, k * W:(k + 1) * W], z3p[:, :, c], K["down"], start=True, stop=True))
                all_drained()
                resample(W, 8, lambda b, k, w: mm(
                    b[0:C, k * H:(k + 1) * H], y13p[:, :, w], K["down"], start=True, stop=True))
                assert job[0] == JOBS
                group_means(1)
                shifts(1, shift_in)
                ph.end()
                pe.wait_ge(pads_ready, img + 1)
                for g in range(HALF):
                    first, count = g * PETAPS[0], PETAPS[g]
                    for k in range(8 + LAG):
                        if k < 8:
                            if 8 * g + k >= 4:
                                pe.wait_ge(in_read, img * 16 + (8 * g + k - 3))
                            mm(bank[k % 4][0:C, :], wins[:, C * g:C * g + C], xT[:, 512 * k:512 * k + 512],
                               start=True, stop=True).then_inc(in_ready, 1)
                        if k >= LAG:
                            r = k - LAG
                            j = 8 * g + r
                            pe.wait_ge(in_read, img * 16 + (8 * g + min(r + 2, 8)))
                            if j >= 4:
                                pe.wait_ge(taps_read, img * 16 + (j - 3))
                            for t in range(count):
                                i = mm(bank[4 + j % 4][0:C, :], diag[:, first + t, :],
                                       xp4p[:, g, 8 * r + t // 3:8 * (r + 1) + t // 3, t % 3:t % 3 + W],
                                       start=(t == 0), stop=(t == count - 1))
                            i.then_inc(taps_ready, 1)

                for o in range(2):
                    n0 = img * (2 * NC) + o * NC
                    m0 = img * (4 * NC) + o * 2 * NC
                    v0 = img * (4 * NC) + o * 2 * NC

                    def chunk_of_u(g, c):
                        return u4p[:, g, c, :] if o == 0 else u4p[:, g, :, c]

                    def bc(b):
                        n = o * (NC // CB) + b
                        if o == 0 and b % 2 == 0:
                            pe.wait_ge(silu_done, img * 8 + min(3 + b, 8))
                        if n >= 2:
                            pe.wait_ge(b_moved, img * (2 * NC // CB) + (n - 1))
                            pe.wait_ge(c_moved, img * (2 * NC // CB) + (n - 1))
                        for g in range(HALF):
                            src = u4p[:, g, CB * b:CB * (b + 1), :] if o == 0 else u4p[:, g, :, CB * b:CB * (b + 1)].rearrange("p h w -> p w h")
                            i = mm(bank[n % 2][:, :], wbc[:, o, g, :], src, start=(g == 0), stop=(g == HALF - 1))
                        i.then_inc(bc_ready, 1)

                    def tokens(t):
                        n = o * (NC // TB) + t
                        if n >= 2:
                            pe.wait_ge(tok_out, img * (2 * NC // TB) + (n - 1))
                        for k in range(TB // 2):
                            for g in range(HALF):
                                for e in range(2):
                                    i = mm(bank[2 + n % 2][Q * e:Q * e + Q, k * 2 * ND:(k + 1) * 2 * ND], chunk_of_u(g, TB * t + 2 * k + e),
                                           wtok[:, o, g, :], start=(g == 0), stop=(g == HALF - 1), skip_group_check=True)
                        i.then_inc(tok_ready, 1)

                    def cb(b):
                        n = o * (NC // CB) + b
                        pe.wait_ge(b_moved, img * (2 * NC // CB) + (n + 1))
                        pe.wait_ge(c_moved, img * (2 * NC // CB) + (n + 1))
                        if n >= 2:
                            pe.wait_ge(g_read, img * (2 * NC // CB) + (n - 1))
                        for k in range(CB):
                            for d in range(2):
                                i = mm(bank[4 + n % 2][Q * d:Q * d + Q, k * Q:(k + 1) * Q], bct[32 * d:32 * d + 32, 0, b % 4, k * Q:(k + 1) * Q],
                                       bct[32 * d:32 * d + 32, 1, b % 4, k * Q:(k + 1) * Q], start=True, stop=True, skip_group_check=True)
                        i.then_inc(g_ready, 1)

                    for b in range(NC // CB):
                        bc(b)
                        for t in range(CB // TB * b, CB // TB * (b + 1)):
                            tokens(t)
                        cb(b)
                    ph.end()
                    pe.wait_ge(aa_ready, img * 2 + (o + 1))
                    mm(bank[0][:, 0:NC * R], K["after"], aa[:, :], start=True, stop=True)
                    mm(bank[1][:, 0:NC * R], K["upto"], aa[:, :], start=True, stop=True)
                    mm(bank[2][0:C, 0:NC * R], K["dirsum"], aa[:, :], start=True, stop=True).then_inc(cum_ready, 1)
                    warm(WARM1)
                    ph.end()

                    def turn_u(base, ubanks):
                        def op(c, s):
                            pe.wait_ge(uc_ready, m0 + (base * NC + c + 1))
                            reuse(pe, up_ready, v0 + base * NC, c, ubanks)
                            apart(pe)
                            for g in range(HALF):
                                i = nc.tensor.transpose(bank[s % ubanks][:, g * C:(g + 1) * C],
                                                        ud[0:C, s % 4, g].rearrange("p k t -> p (k t)"), ident(C))
                            i.then_inc(ut_ready, 1)
                        return op

                    def add_state(c, s):
                        keep_warm()
                        pe.wait_ge(up_ready, v0 + (c + 1))
                        pe.wait_ge(bh_ready, n0 + (c + 1))
                        reuse(pe, dh_read, n0, c, 2)
                        for g in range(HALF):
                            for r in range(RH):
                                h = g * RH + r
                                i = mm(bank[4 + s % 2][32 * r:32 * r + 32, g * DH:(g + 1) * DH], bh[:, s % 4, h, :],
                                       up[:, s % 4, h * DH:(h + 1) * DH], start=True, stop=True)
                        i.then_inc(dh_ready, 1)

                    skewed(pe, 4, [(0, turn_u(0, 4)), (-2, add_state)])
                    ph.end()
                    pe.wait_ge(fwd_scanned, img * 2 + (o + 1))
                    warm(WARM2)
                    ph.end()

                    def log_decay(c, s):
                        pe.wait_ge(r_ready, n0 + (c + 1))
                        reuse(pe, e_ready, n0, c, 2)
                        for k, part in enumerate((r16[:, s % 2, 0, :], r16[:, s % 2, 1, :], zero16[:, 0:192])):
                            i = mm(bank[2 + s % 2][:, 0:R * Q if k < 2 else 192], after16[:, :], part, start=(k == 0), stop=(k == 2))
                        i.then_inc(d_ready, 1)

                    def turn_c(c, s):
                        pe.wait_ge(ct_ready, n0 + (c + 1))
                        reuse(pe, ch_ready, n0, c, 2)
                        for g in range(HALF):
                            i = mm(bank[4 + s % 2][0:C, g * Q:(g + 1) * Q],
                                   ct[:, s % 2, RH * g:RH * g + RH, :].rearrange("p r n -> p (r n)"), K["fold"],
                                   start=True, stop=True)
                        i.then_inc(c_ready, 1)

                    def outputs(c, s):
                        pe.wait_ge(hbd_ready, n0 + (c + 1))
                        pe.wait_ge(ch_ready, n0 + (c + 1))
                        pe.wait_ge(m_ready, n0 + (c + 1))
                        reuse(pe, y_added, n0, c, 2)
                        b = bank[6 + s % 2]
                        for g in range(HALF):
                            mm(b[0:C, g * Q:(g + 1) * Q], hbd[0:C, s % 4, g, :], ch[0:C, s % 4, g, :], start=True, stop=True)
                            for r in range(RH):
                                h = g * RH + r
                                i = mm(b[32 * r:32 * r + 32, g * Q:(g + 1) * Q], up[:, s % 4, h * DH:(h + 1) * DH],
                                       mk[:, s % 2, :].rearrange("p (t r) -> p r t", r=R)[:, h, :], start=False, stop=True, skip_group_check=True)
                        i.then_inc(yc_ready, 1)

                    skewed(pe, 4, [(0, turn_u(1, 2)), (0, log_decay), (0, turn_c), (-2, outputs)])
                    ph.end()
                for q in range(NG):
                    for k in range(GBLK):
                        t0 = 128 * (GBLK * q + k)
                        i = nc.tensor.transpose(bank[q][:, k * C:(k + 1) * C], xT[0:C, t0:t0 + 128], ident(C))
                    i.then_inc(xt_ready, 1)
                pe.wait_ge(xt_act, img * (NG // 2) + NG // 2)
                pe.wait_ge(xt_dve, img * (NG // 2) + NG // 2)
                for n in range(NBLK):
                    b, k = divmod(n, BBLK)
                    for g in range(HALF):
                        mm(bank[b][:, k * (C + 1):(k + 1) * (C + 1)], y[:, g * L + 128 * n:g * L + 128 * n + 128],
                           woutc[:, g, :], start=(g == 0), stop=(g == 1))
                for q in range(4):
                    pe.wait_ge(sq_done, img * 4 + (q + 1))
                    for n in range(NBLK // 4 * q, NBLK // 4 * (q + 1)):
                        i = mm(bank[7][:, n:n + 1], ysq[:, 128 * n:128 * n + 128], K["col192"], start=True, stop=True)
                i.then_inc(fin_ready, 1)
                ph.end()
                assert ph.k == PHASES, ph.k

        @block.scalar
        def _(act):
            ac = nc.scalar.activation
            ph = Phase(act)
            own = Own(act, act_own, 2, 0)
            act.wait_ge(loads, 16 * NLOAD)
            ac(aneg, aneg, ACT.Exp).then_inc(anegexp, 1)
            ph.end()
            with act.Fori(0, images) as img:
                ph.image(img)
                own.image(img)
                for j in range(0, 8, 2):
                    act.wait_ge(tr_ready, img * 8 + (j + 1))
                    ac(xT3[:, :, 8 * j:8 * j + 8].rearrange("p h w -> p w h"),
                       bank[j % 4][0:C, :].rearrange("p (w h) -> p w h", w=8), ACT.Copy).then_inc(tr_act, 1)

                def evacuate(n, dst, src):
                    act.wait_ge(job_ready, img * JOBS + (n + 1))
                    ac(dst, src, ACT.Copy).then_inc(job_act, 1)

                def norm(k):
                    act.wait_ge(var_ready, img * 2 + (k + 1))
                    own(ac(gvar[0:C, :], gvar[0:C, :], ACT.Ln))
                    ac(rstd[0:C, :], gvar[0:C, :], ACT.Exp, scale=-0.5).then_inc(rstd_ready, 1)

                up_columns(0, evacuate)
                up_rows(0, evacuate, {11: lambda: norm(0)})
                ph.end()
                for t in range(NTILE):
                    if t >= 2:
                        act.wait_ge(proj_ready, img * NTILE + (t - 1))
                    for k in range(KH):
                        act.wait_ge(hid_ready, img * (NTILE * KH) + (KH * t + k + 1))
                        ac(sq[:, t % 2, k, :], bank[3 * (t % 2) + k][:, 0:NROW * GRID], ACT.Square,
                           bias=bias1[:, k:k + 1]).then_inc(hid_sq, 1)
                ph.end()
                down_rows(0, evacuate)
                norm(1)
                ph.end()
                act.wait_ge(pads_ready, img + 1)
                def tanh(g, q):
                    act.wait_ge(conv_done, img * 8 + (4 * g + q + 1))
                    part = slice(g * L + q * QUART, g * L + (q + 1) * QUART)
                    ac(etmp[0:C, part], u[0:C, part], ACT.Tanh).then_inc(tanh_done, 1)

                for g in range(HALF):
                    for k in range(8 + LAG):
                        if k < 8:
                            act.wait_ge(in_ready, img * 16 + (8 * g + k + 1))
                            ac(xp4[:, g, 1 + 8 * k:9 + 8 * k, 1:1 + W], bank[k % 4][0:C, :].rearrange("p (h w) -> p h w", h=8),
                               ACT.Identity, bias=biasin[0:C, g:g + 1]).then_inc(in_read, 1)
                        if k >= LAG:
                            r = k - LAG
                            j = 8 * g + r
                            act.wait_ge(taps_ready, img * 16 + (j + 1))
                            ac(u4[:, g, 8 * r:8 * (r + 1), :], bank[4 + j % 4][0:C, :].rearrange("p (h w) -> p h w", h=8),
                               ACT.Identity, bias=bconv[0:C, g:g + 1]).then_inc(taps_read, 1)
                        if g == 1 and k >= 4 + LAG:
                            tanh(0, k - 4 - LAG)
                tanh(1, 0)
                tanh(1, 1)
                for o in range(2):
                    n0 = img * (2 * NC) + o * NC
                    v0 = img * (4 * NC) + o * 2 * NC

                    def tokens_out(t):
                        n = o * (NC // TB) + t
                        act.wait_ge(tok_ready, img * (2 * NC // TB) + (n + 1))
                        for d in range(2):
                            for e in range(2):
                                i = ac(tok3[Q * d:Q * d + Q, TB * t + e:TB * t + TB - 1 + e:2, (NT - ND) * d:(NT - ND) * d + ND],
                                       bank[2 + n % 2][Q * e:Q * e + Q, 0:TB * ND].rearrange("p (c n) -> p c n", c=TB // 2)
                                       [:, :, ND * d:ND * d + ND], ACT.Copy)
                        i.then_inc(tok_out, 1)

                    def copy_u_twice(first):
                        def op(c, s):
                            reuse(act, ut_ready, first, c, 4)
                            ac(ud[0:C, s % 4], chunk(u4, o, c).unsqueeze(2).broadcast_to((C, HALF, 2, Q)),
                               ACT.Copy).then_inc(uc_ready, 1)
                        return op

                    for b in range(NC // CB):
                        n = o * (NC // CB) + b
                        act.wait_ge(bc_ready, img * (2 * NC // CB) + (n + 1))
                        if b >= 4:
                            act.wait_ge(g_ready, img * (2 * NC // CB) + (n - 3))
                        ac(bct[0:64, 0, b % 4], bank[n % 2][0:64, :], ACT.Copy).then_inc(b_moved, 1)
                        if o == 0 and b < 2:
                            ac(bct[0:64, 1, b % 4], bank[n % 2][64:128, :], ACT.Copy).then_inc(c_moved, 1)
                        for t in range(CB // TB * b, CB // TB * (b + 1)):
                            tokens_out(t)
                        if o == 0 and b == 1:
                            tanh(1, 2)
                            tanh(1, 3)
                    ph.end()
                    act.wait_ge(abs_ready, img * 2 + (o + 1))
                    ac(expn[:, :], expn[:, :], ACT.Exp, scale=-1.0).then_inc(spe_ready, 1)
                    act.wait_ge(onep_ready, img * 2 + (o + 1))
                    ac(dt[:, :], onep[:, :], ACT.Ln).then_inc(ln_ready, 1)
                    act.wait_ge(cum_ready, img * 2 + (o + 1))
                    ac(tot[0:C, :], bank[2][0:C, 0:NC * R], ACT.Exp)
                    ac(wsuf[:, :], bank[0][:, 0:NC * R], ACT.Exp)
                    ac(ecum[:, :], bank[1][:, 0:NC * R], ACT.Exp).then_inc(cum_exp, 1)
                    ph.end()

                    def state_in(c, s):
                        act.wait_ge(dh_ready, n0 + (c + 1))
                        ac(states(hb)[:, :, one(c + 1)], bank[4 + s % 2][0:C, 0:HALF * DH].unsqueeze(2),
                           ACT.Copy).then_inc(dh_read, 1)

                    skewed(act, 4, [(2, copy_u_twice(v0)), (-3, state_in)])
                    ph.end()
                    def skip_term(g):
                        ac(y[0:C, g * L:(g + 1) * L], u[0:C, g * L:(g + 1) * L], ACT.Copy, scale=dsum[0:C, g:g + 1])

                    if o == 0:
                        skip_term(0)
                    else:
                        ac(xT[0:C, :], xT[0:C, :], ACT.Identity, bias=bcol[0:C, 0:1])
                    act.wait_ge(fwd_scanned, img * 2 + (o + 1))
                    ac(hf[0:C, 0:NST - 2], hf[0:C, 0:NST - 2], ACT.Copy, scale=K["fwd"][0:C, :]).then_inc(fwd_masked, 1)
                    if o == 0:
                        skip_term(1)
                    ph.end()

                    def decay(c, s):
                        act.wait_ge(d_ready, n0 + (c + 1))
                        reuse(act, m_ready, n0, c, 2)
                        ac(ee[:, s % 2, :], bank[2 + s % 2][:, 0:R * Q], ACT.Exp).then_inc(e_ready, 1)

                    def c_in(c, s):
                        act.wait_ge(c_ready, n0 + (c + 1))
                        reuse(act, yc_ready, n0, c, 4)
                        ac(ch[0:C, s % 4], bank[4 + s % 2][0:C, 0:HALF * Q].rearrange("p (g t) -> p g t", g=HALF),
                           ACT.Copy).then_inc(ch_ready, 1)

                    skewed(act, 4, [(2, copy_u_twice(v0 + NC)), (0, decay), (0, c_in)])
                    ph.end()
                act.sem_inc(u_free, 1)
                for q in range(0, NG, 2):
                    act.wait_ge(xt_ready, img * NG + (q + 1))
                    ac(ot[:, q * GBLK * C:(q + 1) * GBLK * C], bank[q][:, 0:GBLK * C], ACT.Copy).then_inc(xt_act, 1)
                for q in range(4):
                    ac(ysq[0:C, :].rearrange("p (g t) -> p g t", g=HALF)[:, :, QUART * q:QUART * (q + 1)],
                       y[0:C, :].rearrange("p (g t) -> p g t", g=HALF)[:, :, QUART * q:QUART * (q + 1)],
                       ACT.Square).then_inc(sq_ready, 1)
                act.wait_ge(fin_var, img + 1)
                ac(rstds[:, 2, :], rstds[:, 1, :], ACT.Ln).then_inc(fin_ln, 1)
                act.wait_ge(fin_ln, img + 1)
                ac(rstds[:, 3, :], rstds[:, 2, :], ACT.Exp, scale=-0.5).then_inc(fin_rstd, 1)
                ph.end()
                assert ph.k == PHASES and own.n == 2

        @block.gpsimd
        def _(pool):
            tt = nc.gpsimd.tensor_tensor
            ph = Phase(pool)
            nc.gpsimd.memset(arena[C:128, 0:QUIET], 0.0)
            nc.gpsimd.memset(xs[W:C, :], 0.0)
            for t in (xT, wins, diag.rearrange("p k c -> p (k c)"), wbc.rearrange("p o g n -> p (o g n)"),
                      wtok.rearrange("p o g n -> p (o g n)"), woutc.rearrange("p g c -> p (g c)")):
                i = nc.gpsimd.memset(t[C:128], 0.0)
            ph.end()
            with pool.Fori(0, images) as img:
                ph.image(img)
                apart(pool)
                nc.gpsimd.memset(st_a[W:C, :], 0.0).then_inc(st_padded, 1)
                for _ in range(3):
                    ph.end()
                apart(pool)
                for g in range(HALF):
                    nc.gpsimd.memset(xp4[:, g, 0:PW:PW - 1, :], 0.0)
                    i = nc.gpsimd.memset(xp4[:, g, 1:PW - 1, 0:PW:PW - 1], 0.0)
                i.then_inc(pads_ready, 1)
                for o in range(2):
                    n0 = img * (2 * NC) + o * NC

                    ph.end()
                    ph.end()

                    def token_values(c, col):
                        v = tok3[:, one(c), :]
                        both = bass.AP(v.tensor, v.offset + col, [v.ap[0], [0, R], [NT - N * 2, 2], [1, N]])
                        return both

                    def weigh(dst, ring, weight, col):
                        def op(c, s):
                            return tt(dst[:, s % ring].rearrange("p r (d n) -> p r d n", d=2), rc(weight)[:, one(c), :].rearrange("p c r -> p (c r)").unsqueeze(2)
                                      .unsqueeze(3).broadcast_to((128, R, 2, N)),
                                      token_values(c, col), ALU.mult)
                        return op

                    def weigh_b(c, s):
                        reuse(pool, dh_ready, n0, c, 4)
                        weigh(bh, 4, wsuf, 0)(c, s).then_inc(bh_ready, 1)

                    skewed(pool, 4, [(0, weigh_b)])
                    ph.end()
                    ph.end()

                    def weigh_c(c, s):
                        reuse(pool, c_ready, n0, c, 2)
                        weigh(ct, 2, ecum, N)(c, s).then_inc(ct_ready, 1)

                    def state_out(c, s):
                        reuse(pool, yc_ready, n0, c, 4)
                        tt(hbd[0:C, s % 4].rearrange("p g (r d) -> p r g d", r=RH),
                           states(hf)[:, :, one(c)].rearrange("p (g d) c -> p c g d", g=HALF).broadcast_to((C, RH, HALF, DH)),
                           K["headsel"][0:C, :].unsqueeze(2).unsqueeze(3).broadcast_to((C, RH, HALF, DH)),
                           ALU.mult).then_inc(hbd_ready, 1)

                    skewed(pool, 4, [(0, weigh_c), (0, state_out)])
                    ph.end()
                apart(pool)
                nc.gpsimd.memset(xs[W:C, :], 0.0)
                ph.end()
                assert ph.k == PHASES

        @block.vector
        def _(dve):
            v = nc.vector
            ph = Phase(dve)
            PRO, PER = 7, 87
            own = Own(dve, dve_own, PER, PRO)
            dve.wait_ge(loads, 16 * NLOAD)
            for k in range(KH):
                v.tensor_scalar(w2s[:, k, :], w2t[:, k, :], coef[:, k, 2:3], None, ALU.mult)
                v.tensor_scalar(w2l[:, k, :], w2t[:, k, :], coef[:, k, 1:2], None, ALU.mult)
                v.scalar_tensor_tensor(vconst[:, k:k + 1], b1[:, k:k + 1], coef[:, k, 1:2], coef[:, k, 0:1], ALU.mult, ALU.add)
            for g in range(HALF):
                v.tensor_scalar(woutc[0:C, g, 0:C], wout[0:C, g, :], lng[0:C, g:g + 1], None, ALU.mult)
            v.memset(woutc[0:C, :, C:C + 1], 1.0 / DI)
            v.tensor_reduce(dsum[0:C, :], dsk[0:C], mybir.AxisListType.X, ALU.add).then_inc(w2_scaled, 1)
            v.tensor_scalar(bconv[0:C, :], bconv[0:C, :], 0.5, None, ALU.mult)
            own(v.tensor_scalar(wconv[0:C], wconv[0:C], 0.5, None, ALU.mult))
            for g in range(HALF):
                for t in range(PETAPS[g]):
                    v.tensor_scalar(diag[0:C, g * PETAPS[0] + t, :], K["ident"][0:C, 0:C], wconv[0:C, g, t:t + 1], None, ALU.mult)
            v.tensor_copy(after16[:, :], K["after"])
            v.memset(zero16[:, :], 0.0)
            v.tensor_copy(tri16[:, :].rearrange("p (t r) -> p t r", r=R), K["tri"].unsqueeze(2).broadcast_to((128, Q, R)))
            dve.wait_ge(anegexp, 1)
            own(v.tensor_scalar(aneg, aneg, -1.0, None, ALU.mult))
            dve.wait_ge(folded, 1)
            own(v.tensor_copy(lin[0:C, :], bank[0][0:C, 0:C]))
            own(v.tensor_tensor(out0[0:C, :], bank[1][0:C, 0:1], b2[0:C, :], ALU.add))
            for g in range(HALF):
                own(v.tensor_tensor(woutc[0:C, g, 0:C], woutc[0:C, g, 0:C], bank[2][0:C, 0:C], ALU.subtract))
            own(v.tensor_copy(bcol[0:C, :], bank[3][0:C, 0:1]))
            ph.end()
            with dve.Fori(0, images) as img:
                ph.image(img)
                own.image(img)

                def evacuate(n, dst, src):
                    dve.wait_ge(job_ready, img * JOBS + (n + 1))
                    v.tensor_copy(dst, src).then_inc(job_dve, 1)

                def stats(j):
                    return v.bn_stats(bn[0:C, j, :], xT3[:, :, 8 * j:8 * j + 8])

                def moments(i):
                    own(i)
                    apart(dve)
                    own(v.bn_aggr(mv[0:C, :], bn[0:C]))
                    v.tensor_copy(mom[0:C, 0:1], mv[0:C, 0:1])
                    v.scalar_tensor_tensor(mom[0:C, 1:2], mv[0:C, 0:1], mv[0:C, 0:1], mv[0:C, 1:2],
                                           ALU.mult, ALU.add).then_inc(mom_ready, 1)

                def variance(k):
                    dve.wait_ge(grp_ready, img * 2 + (k + 1))
                    own(v.tensor_copy(gst[0:C, :], bank[0][0:C, 0:2]))
                    own(v.tensor_tensor(gsq[0:C, :], gst[0:C, 0:1], gst[0:C, 0:1], ALU.mult))
                    own(v.tensor_tensor(gvar[0:C, :], gst[0:C, 1:2], gsq[0:C, :], ALU.subtract))
                    v.tensor_scalar(gvar[0:C, :], gvar[0:C, :], 0.0, 1e-5, ALU.max, ALU.add).then_inc(var_ready, 1)

                def shift(k):
                    dve.wait_ge(rstd_ready, img * 2 + (k + 1))
                    v.scalar_tensor_tensor(nmr[0:C, :], gst[0:C, 0:1], -1.0, rstd[0:C, :],
                                           ALU.mult, ALU.mult).then_inc(nmr_ready, 1)

                def scale_w1():
                    shift(0)
                    v.tensor_scalar(w1s[0:C, :], w1t[0:C, :], rstd[0:C, 0:1], None, ALU.mult)
                    v.tensor_scalar(lins[0:C, :], lin[0:C, :], rstd[0:C, 0:1], None, ALU.mult)

                def bias_layer0():
                    dve.wait_ge(shift_ready, img * 2 + 1)
                    v.tensor_tensor(bias1[:, :], bank[1][:, 0:KH], b1[:, :], ALU.add)
                    v.tensor_tensor(out0i[0:C, :], bank[1][0:C, KH:KH + 1], out0[0:C, :], ALU.add)

                for j in range(1, 8, 2):
                    dve.wait_ge(tr_ready, img * 8 + (j + 1))
                    v.tensor_copy(xT3[:, :, 8 * j:8 * j + 8].rearrange("p h w -> p w h"),
                                  bank[j % 4][0:C, :].rearrange("p (w h) -> p w h", w=8)).then_inc(tr_dve, 1)
                dve.wait_ge(tr_act, img * 4 + 4)
                dve.wait_ge(tr_dve, img * 4 + 4)
                up_columns(1, evacuate, {2 * j + 1: (lambda j=j: stats(j)) for j in range(7)})
                moments(stats(7))
                up_rows(1, evacuate, {10: lambda: variance(0), 14: scale_w1, 18: bias_layer0})
                ph.end()
                for t in range(NTILE):
                    dve.wait_ge(proj_ready, img * NTILE + (t + 1))
                    v.tensor_copy(z3[:, NROW * t:NROW * (t + 1), :],
                                  bank[6 + t % 2][0:GRID, 0:NROW * C].rearrange("p (h c) -> p h c", h=NROW)).then_inc(proj_read, 1)
                ph.end()
                down_rows(1, evacuate)
                i = down_columns(img, dve, v, stats)
                moments(i)
                variance(1)
                shift(1)
                own(v.tensor_scalar(wins[0:C, :], win[0:C, :], rstd[0:C, 0:1], None, ALU.mult))
                dve.wait_ge(shift_ready, img * 2 + 2)
                own(v.tensor_copy(biasin[0:C, :], bank[1][0:C, 0:HALF]))
                ph.end()
                v.memset(tok3[0:Q, :, ND:NT], 0.0)
                v.memset(tok3[Q:128, :, 0:NT - ND], 0.0)

                def taps(g, q):
                    dve.wait_ge(taps_read, img * 16 + (8 * g + 2 * q + 2))
                    for t in range(PETAPS[g], 9):
                        src = xp4[:, g, 16 * q + t // 3:16 * (q + 1) + t // 3, t % 3:t % 3 + W]
                        dst = u4[:, g, 16 * q:16 * (q + 1), :]
                        i = v.scalar_tensor_tensor(dst, src, wconv[0:C, g, t:t + 1], dst, ALU.mult, ALU.add)
                        if t < 8:
                            own(i)
                        else:
                            i.then_inc(conv_done, 1)

                def silu(g, q):
                    dve.wait_ge(tanh_done, img * 8 + (4 * g + q + 1))
                    part = slice(g * L + q * QUART, g * L + (q + 1) * QUART)
                    v.scalar_tensor_tensor(u[0:C, part], etmp[0:C, part], 1.0, u[0:C, part],
                                           ALU.add, ALU.mult).then_inc(silu_done, 1)

                for q in range(4):
                    dve.wait_ge(in_read, img * 16 + min(2 * q + 3, 8))
                    taps(0, q)
                for q in range(4):
                    dve.wait_ge(in_read, img * 16 + (8 + min(2 * q + 3, 8)))
                    taps(1, q)
                    silu(0, q)
                    if q:
                        silu(1, q - 1)
                silu(1, 3)
                dve.wait_ge(stored, img * 16 + 16)
                for o in range(2):
                    n0 = img * (2 * NC) + o * NC
                    v0 = img * (4 * NC) + o * 2 * NC

                    def mask_g(b):
                        n = o * (NC // CB) + b
                        dve.wait_ge(g_ready, img * (2 * NC // CB) + (n + 1))
                        v.tensor_tensor(gm3[:, CB * b:CB * (b + 1), :], bank[4 + n % 2][:, :].rearrange("p (c t) -> p c t", c=CB),
                                        K["tri"].unsqueeze(1).broadcast_to((128, CB, Q)), ALU.mult).then_inc(g_read, 1)

                    for b in range(NC // CB):
                        n = o * (NC // CB) + b
                        if o == 1 or b >= 2:
                            dve.wait_ge(bc_ready, img * (2 * NC // CB) + (n + 1))
                            if b >= 4:
                                dve.wait_ge(g_ready, img * (2 * NC // CB) + (n - 3))
                            v.tensor_copy(bct[0:64, 1, b % 4], bank[n % 2][64:128, :]).then_inc(c_moved, 1)
                        if b:
                            mask_g(b - 1)
                    mask_g(NC // CB - 1)
                    ph.end()
                    own(v.tensor_tensor(rc(dtraw), tok3[:, :, 2 * N:2 * N + R], dtb[:, o, :].unsqueeze(1).broadcast_to((128, NC, R)), ALU.add))
                    v.scalar_tensor_tensor(expn[:, :], dtraw[:, :], -1.0, dtraw[:, :], ALU.mult, ALU.max).then_inc(abs_ready, 1)
                    dve.wait_ge(spe_ready, img * 2 + (o + 1))
                    v.tensor_scalar(onep[:, :], expn[:, :], 1.0, None, ALU.add).then_inc(onep_ready, 1)
                    dve.wait_ge(onep_ready, img * 2 + (o + 1))
                    own(v.tensor_scalar(den[:, :], onep[:, :], -1.0, None, ALU.add))
                    own(v.tensor_scalar(tiny[:, :], den[:, :], 0.0, None, ALU.is_equal))
                    own(v.tensor_tensor(den[:, :], den[:, :], tiny[:, :], ALU.add))
                    own(v.reciprocal(den[:, :], den[:, :]))
                    own(v.tensor_tensor(den[:, :], den[:, :], expn[:, :], ALU.mult))
                    own(v.tensor_tensor(tiny[:, :], tiny[:, :], expn[:, :], ALU.mult))
                    dve.wait_ge(ln_ready, img * 2 + (o + 1))
                    own(v.tensor_tensor(dt[:, :], dt[:, :], den[:, :], ALU.mult))
                    own(v.tensor_tensor(dt[:, :], dt[:, :], tiny[:, :], ALU.add))
                    own(v.scalar_tensor_tensor(dt[:, :], dtraw[:, :], 0.0, dt[:, :], ALU.max, ALU.add))
                    v.tensor_tensor(rc(aa), rc(dt), aneg[:, o, :].unsqueeze(1).broadcast_to((128, NC, R)),
                                    ALU.mult).then_inc(aa_ready, 1)
                    dve.wait_ge(aa_ready, img * 2 + (o + 1))
                    own(v.tensor_scalar(aclip[:, :], aa[:, :], -1000.0, None, ALU.max))
                    own(v.tensor_copy(a16[:, 0, :], aclip[:, :]))
                    v.tensor_tensor(a16[:, 1, :], aclip[:, :], a16[:, 0, :], ALU.subtract)
                    dve.wait_ge(cum_exp, img * 2 + (o + 1))
                    own(v.tensor_tensor(tot[0:C, :].rearrange("p (n r) -> p n r", r=RH), tot[0:C, :].rearrange("p (n r) -> p n r", r=RH),
                                        K["headsel"][0:C, :].unsqueeze(1).broadcast_to((C, HALF * NC, RH)), ALU.mult))
                    own(v.tensor_reduce(dec[0:C, :], tot[0:C, :].rearrange("p (n r) -> p n r", r=RH), mybir.AxisListType.X, ALU.add))
                    ph.end()

                    def scale_u(phase, ubanks):
                        def op(c, s):
                            dve.wait_ge(ut_ready, v0 + (phase * NC + c + 1))
                            reuse(dve, dh_ready if phase == 0 else yc_ready, n0, c, 4)
                            v.tensor_tensor(up[:, s % 4].rearrange("p (r d) -> p r d", r=R),
                                            bank[s % ubanks][:, 0:R * DH].rearrange("p (r d) -> p r d", r=R),
                                            rc(dt)[:, one(c), :].rearrange("p c r -> p (c r)").unsqueeze(2).broadcast_to((128, R, DH)),
                                            ALU.mult).then_inc(up_ready, 1)
                        return op

                    skewed(dve, 4, [(0, scale_u(0, 4))])
                    v.memset(states(decx)[:, :, 0:1], 0.0)
                    v.memset(decx[0:C, NST - 1:NST], 0.0)
                    v.memset(states(hb)[:, :, 0:1], 0.0)
                    v.memset(hb[0:C, NST - 1:NST], 0.0)
                    dec3 = dec[0:C, :].rearrange("p (c g) -> p g c", g=HALF)
                    for g in range(HALF):
                        v.tensor_copy(states(decx)[:, g * DH:(g + 1) * DH, 1:SLOT],
                                      dec3[:, g:g + 1, :].broadcast_to((C, DH, NC)))
                    ph.end()
                    v.tensor_tensor_scan(hf[0:C, :], decx[0:C, :], hb[0:C, :], 0.0, ALU.mult, ALU.add).then_inc(fwd_scanned, 1)
                    dve.wait_ge(fwd_scanned, img * 2 + (o + 1))
                    own(v.tensor_tensor_scan(hb[0:C, ::-1], decx[0:C, ::-1], hb[0:C, ::-1], 0.0, ALU.mult, ALU.add))
                    dve.wait_ge(fwd_masked, img * 2 + (o + 1))
                    own(v.scalar_tensor_tensor(hf[0:C, 0:NST - 2], hb[0:C, 2:NST], K["bwd"][0:C, :], hf[0:C, 0:NST - 2],
                                               ALU.mult, ALU.add))
                    ph.end()

                    def spread_a(c, s):
                        reuse(dve, d_ready, n0, c, 2)
                        i = v.tensor_tensor(r16[:, s % 2].rearrange("p k (t r) -> p k t r", r=R),
                                            a16[:, :, bass.ds(R * c, R) if not isinstance(c, int) else slice(R * c, R * c + R)]
                                            .unsqueeze(2).broadcast_to((128, 2, Q, R)),
                                            tri16[:, :].rearrange("p (t r) -> p t r", r=R).unsqueeze(1).broadcast_to((128, 2, Q, R)),
                                            ALU.mult)
                        i.then_inc(r_ready, 1)

                    def weigh_g(c, s):
                        dve.wait_ge(e_ready, n0 + (c + 1))
                        reuse(dve, yc_ready, n0, c, 2)
                        v.tensor_tensor(mk[:, s % 2].rearrange("p (t r) -> p t r", r=R), ee[:, s % 2].rearrange("p (t r) -> p t r", r=R),
                                        gm3[:, one(c), :].rearrange("p c t -> p (c t)").unsqueeze(2).broadcast_to((128, Q, R)),
                                        ALU.mult).then_inc(m_ready, 1)

                    def add_y(c, s):
                        dve.wait_ge(yc_ready, n0 + (c + 1))
                        yy = chunk(y4, o, c)
                        v.tensor_tensor(yy, yy, bank[6 + s % 2][0:C, 0:HALF * Q].rearrange("p (g t) -> p g t", g=HALF),
                                        ALU.add).then_inc(y_added, 1)

                    skewed(dve, 4, [(1, spread_a), (0, scale_u(1, 2)), (-1, weigh_g), (-3, add_y)])
                    ph.end()

                for q in range(1, NG, 2):
                    dve.wait_ge(xt_ready, img * NG + (q + 1))
                    v.tensor_copy(ot[:, q * GBLK * C:(q + 1) * GBLK * C], bank[q][:, 0:GBLK * C]).then_inc(xt_dve, 1)
                for q in range(4):
                    dve.wait_ge(sq_ready, img * 4 + (q + 1))
                    v.tensor_tensor(ysq[0:C, QUART * q:QUART * (q + 1)], ysq[0:C, QUART * q:QUART * (q + 1)],
                                    ysq[0:C, L + QUART * q:L + QUART * (q + 1)], ALU.add).then_inc(sq_done, 1)
                dve.wait_ge(fin_ready, img + 1)
                for b in range(-(-NBLK // BBLK)):
                    k = min(BBLK, NBLK - b * BBLK)
                    i = v.tensor_copy(rstds[:, 0, b * BBLK:b * BBLK + k], bank[b][:, C:(k - 1) * (C + 1) + C + 1:C + 1])
                own(i)
                own(v.tensor_tensor(rstds[:, 0, :], rstds[:, 0, :], rstds[:, 0, :], ALU.mult))
                own(v.tensor_tensor(rstds[:, 1, :], bank[7][:, 0:NBLK], rstds[:, 0, :], ALU.subtract))
                v.tensor_scalar(rstds[:, 1, :], rstds[:, 1, :], 0.0, 1e-5, ALU.max, ALU.add).then_inc(fin_var, 1)
                dve.wait_ge(fin_rstd, img + 1)
                dve.wait_ge(xt_act, img * (NG // 2) + NG // 2)
                for n in range(NBLK):
                    b, k = divmod(n, BBLK)
                    o_ = ot[:, n * C:(n + 1) * C]
                    v.scalar_tensor_tensor(o_, bank[b][:, k * (C + 1):k * (C + 1) + C], rstds[:, 3, n:n + 1], o_,
                                           ALU.mult, ALU.add).then_inc(fin_done, 1)
                ph.end()
                assert ph.k == PHASES and own.n == PRO + PER, own.n

    return nc


def constants():
    import numpy as np

    theta = 2 * np.pi * (np.arange(GRID) + 0.25) / GRID
    pos = 2 * np.pi * np.arange(W) / W
    freq = np.arange(-W // 2, W // 2 + 1)
    phase = np.exp(1j * freq[:, None, None] * (theta[None, :, None] - pos[None, None, :]))
    edge = np.where(abs(freq) == W // 2, 0.5, 1.0)[:, None, None]
    col = {
        "up": (phase.sum(0).real / W).T,
        "down": (phase * edge).sum(0).real / GRID,
        "ident": np.eye(128),
        "fold": np.tile(np.eye(Q), (2, 1)),
    }
    j = np.arange(Q)
    two = np.zeros((2, Q, 2, Q))
    two[0, :, 0] = j[:, None] > j[None, :]
    two[1, :, 1] = j[:, None] < j[None, :]
    col["after"] = two.reshape(128, 128)
    two = np.zeros((2, Q, 2, Q))
    two[0, :, 0] = j[:, None] <= j[None, :]
    two[1, :, 1] = j[:, None] >= j[None, :]
    col["upto"] = two.reshape(128, 128)
    col["tri"] = np.concatenate([two[0, :, 0], two[1, :, 1]])
    p = np.arange(C)
    direction = p % (2 * N) // N
    col["dirsum"] = np.repeat(np.arange(2), Q)[:, None] == direction[None, :]
    col["group"] = (p[:, None] // GROUP == p[None, :] // GROUP) / GROUP
    col["headsel"] = p[:, None] // (2 * N) == np.arange(RH)[None, :]
    col["fwd"] = (direction == 0)[:, None]
    col["bwd"] = (direction == 1)[:, None]
    col["mean192"] = np.full((C, C), 1.0 / DI)
    col["col192"] = np.full((C, 1), 1.0 / DI)
    out = np.zeros((128, CONST_N), np.float32)
    for name, v in col.items():
        s, e = CONST_AT[name]
        assert v.shape[1] == e - s, name
        out[:v.shape[0], s:e] = v
    return out


def laid_out(inputs):
    import numpy as np

    i = {k: np.asarray(v) for k, v in inputs.items()}
    xp = i["L1_conv_x_proj_weight"]
    wtok = np.zeros((2, DI, 2 * ND), np.float32)
    wbc = np.zeros((2, DI, 128), np.float32)
    for o in range(2):
        for d in range(2):
            w = xp[o + 2 * d].T
            wtok[o, :, 2 * N + R * d:2 * N + R * (d + 1)] = w[:, 0:R]
            wtok[o, :, (2 * N + 2 * R) * d:(2 * N + 2 * R) * d + 2 * N] = w[:, R:]
            wbc[o, :, 32 * d:32 * d + N] = w[:, R:R + N]
            wbc[o, :, 64 + 32 * d:64 + 32 * d + N] = w[:, R + N:R + 2 * N]

    def cols(v, p):
        return v.reshape(-1, p).T

    arrays = {
        "x": i["x"], "consts": constants(), "W1": i["L0_conv_W1"], "W1T": i["L0_conv_W1"].T, "W2T": i["L0_conv_W2"].T,
        "b1": cols(i["L0_conv_b1"], 128), "b2": cols(i["L0_conv_b2"], C), "coef": i["L0_conv_coef"], "w_in": i["L1_conv_w_in"],
        "w_conv": i["L1_conv_w_conv"].reshape(9, DI).T, "b_conv": cols(i["L1_conv_b_conv"], C), "wtok": wtok, "wbc": wbc,
        "A_logs": i["L1_conv_A_logs"], "dt_bias": i["L1_conv_dt_bias"], "Ds": i["L1_conv_Ds"].reshape(4, DI).T,
        "ln_g": cols(i["L1_conv_ln_g"], C), "ln_b": cols(i["L1_conv_ln_b"], C), "w_out": i["L1_conv_w_out"],
    }
    return {f"in_{k}": np.ascontiguousarray(v) for k, v in arrays.items()}


def kernel(**inputs):
    import concourse.bacc as bacc
    from concourse.bass_utils import run_bass_kernel_spmd

    nc = bacc.Bacc("TRN2", target_bir_lowering=False, num_devices=1)
    arrays = laid_out(inputs)
    aps = {k[3:]: nc.dram_tensor(k, v.shape, mybir.dt.from_np(v.dtype), kind="ExternalInput").ap() for k, v in arrays.items()}
    out = nc.dram_tensor("out", (B, H, W, C), F32, kind="ExternalOutput").ap()
    build(nc, aps, out)
    r = run_bass_kernel_spmd(nc, [arrays], core_ids=[0])
    return r.results[0]["out"]
```
